# Optimizing a Trainium2 kernel written in Bass

```python
import numpy as np
import jax
import jax.numpy as jnp

def _softmax(x, axis=-1):
    return jax.nn.softmax(x, axis=axis)

def _gelu(x):
    return jax.nn.gelu(x, approximate=True)

def _silu(x):
    return jax.nn.silu(x)

def _sigmoid(x):
    return jax.nn.sigmoid(x)

def _layernorm(x, axis=-1, eps=1e-05):
    m = jnp.mean(x, axis=axis, keepdims=True)
    v = jnp.var(x, axis=axis, keepdims=True)
    return (x - m) / jnp.sqrt(v + eps)

def _scatter_add(tgt, idx, src, axis=0):
    return tgt.at[idx].add(src)

def _segment_sum(src, seg, n):
    return jax.ops.segment_sum(src, seg, n)
kernel_name = 'mk_seq_postln_d1_jaxref_r4_642d9f'

def setup_inputs(seed: int=0):
    np.random.seed(seed)
    _w = jnp.asarray

    def _L0_attn_setup():
        import jax, jax.numpy as jnp
        import numpy as np
        B, T, C, H = (4, 1024, 512, 16)
        Dh = C // H

        def _feature_map(x):
            return jax.nn.elu(x) + 1.0
        key = jax.random.key(seed)
        ks = jax.random.split(key, 7)
        s = 0.02
        return {'x': jax.random.normal(ks[0], (B, T, C), dtype=jnp.float32), 'cos': jax.random.uniform(ks[1], (T, Dh), dtype=jnp.float32), 'sin': jax.random.uniform(ks[2], (T, Dh), dtype=jnp.float32), 'Wq': jax.random.normal(ks[3], (C, C), dtype=jnp.float32) * s, 'Wk': jax.random.normal(ks[4], (C, C), dtype=jnp.float32) * s, 'Wv': jax.random.normal(ks[5], (C, C), dtype=jnp.float32) * s, 'Wo': jax.random.normal(ks[6], (C, C), dtype=jnp.float32) * s}
    _L0_attn_in = _L0_attn_setup()

    def _L0_ffn_setup():
        import jax, jax.numpy as jnp
        import numpy as np
        B, S, D, E, TOPK = (4, 512, 512, 8, 2)
        key = jax.random.key(seed)
        k1, k2, k3 = jax.random.split(key, 3)
        x = jax.random.normal(k1, (B, S, D), dtype=jnp.float32)
        gate_w = jax.random.normal(k2, (E, D), dtype=jnp.float32) * 0.02
        expert_w = jax.random.normal(k3, (E, D, D), dtype=jnp.float32) / np.sqrt(D)
        expert_b = jnp.zeros((E, D), dtype=jnp.float32)
        return {'x': x, 'gate_w': gate_w, 'expert_w': expert_w, 'expert_b': expert_b}
    _L0_ffn_in = _L0_ffn_setup()
    _d = {'L0_attn_x': _L0_attn_in['x'], 'L0_attn_cos': _L0_attn_in['cos'], 'L0_attn_sin': _L0_attn_in['sin'], 'L0_attn_Wq': _L0_attn_in['Wq'], 'L0_attn_Wk': _L0_attn_in['Wk'], 'L0_attn_Wv': _L0_attn_in['Wv'], 'L0_attn_Wo': _L0_attn_in['Wo'], 'L0_ffn_gate_w': _L0_ffn_in['gate_w'], 'L0_ffn_expert_w': _L0_ffn_in['expert_w'], 'L0_ffn_expert_b': _L0_ffn_in['expert_b']}
    _x0 = _d['L0_attn_x']
    _d['L0_attn_x'] = jax.random.normal(jax.random.fold_in(jax.random.key(seed), 1), (4, 512, 512), dtype=_x0.dtype)
    del _x0
    return _d

def reference(L0_attn_x, L0_attn_cos, L0_attn_sin, L0_attn_Wq, L0_attn_Wk, L0_attn_Wv, L0_attn_Wo, L0_ffn_gate_w, L0_ffn_expert_w, L0_ffn_expert_b):

    def _L0_attn_ref(x, cos, sin, Wq, Wk, Wv, Wo):
        import jax, jax.numpy as jnp
        import numpy as np
        B, T, C, H = (4, 1024, 512, 16)
        Dh = C // H

        def _feature_map(x):
            return jax.nn.elu(x) + 1.0
        b, t, c = x.shape
        h, dh = (H, c // H)

        def proj(W):
            y = jnp.einsum('btc,oc->bto', x, W)
            return y.reshape(b, t, h, dh).transpose(0, 2, 1, 3)
        q = _feature_map(proj(Wq))
        k = _feature_map(proj(Wk))
        v = proj(Wv)
        kv = jnp.einsum('bhtd,bhte->bhde', k, v)
        z = 1.0 / (jnp.einsum('bhtd,bhd->bht', q, k.sum(axis=2)) + 1e-06)
        out = jnp.einsum('bhtd,bhde,bht->bhte', q, kv, z)
        out = out.transpose(0, 2, 1, 3).reshape(b, t, c)
        return jnp.einsum('btc,oc->bto', out, Wo)

    def _L0_ffn_ref(x, gate_w, expert_w, expert_b):
        import jax, jax.numpy as jnp
        import numpy as np
        B, S, D, E, TOPK = (4, 512, 512, 8, 2)
        batch_shape = x.shape[:-1]
        xf = x.reshape(-1, x.shape[-1])
        T = xf.shape[0]
        logits = jnp.einsum('td,ed->te', xf, gate_w)
        top_w, top_i = jax.lax.top_k(logits, TOPK)
        top_w = jax.nn.softmax(top_w.astype(jnp.float32), axis=-1).astype(x.dtype)
        gates = jnp.zeros((T, logits.shape[-1]), dtype=x.dtype)
        gates = gates.at[jnp.arange(T)[:, None], top_i].set(top_w)
        y = jnp.einsum('td,edo->eto', xf, expert_w) + expert_b[:, None, :]
        out = jnp.einsum('te,eto->to', gates, y)
        return out.reshape(*batch_shape, -1)
    x = L0_attn_x
    x = _layernorm(x + _L0_attn_ref(x, L0_attn_cos, L0_attn_sin, L0_attn_Wq, L0_attn_Wk, L0_attn_Wv, L0_attn_Wo), axis=-1)
    x = _layernorm(x + _L0_ffn_ref(x, L0_ffn_gate_w, L0_ffn_expert_w, L0_ffn_expert_b), axis=-1)
    return x

_drawn_inputs = setup_inputs


def setup_inputs(seed=0):
    import zlib

    import numpy as np

    out = dict(_drawn_inputs(seed))
    spreads = {'L0_ffn_expert_b': (0.0, 0.1)}
    factors = {'L0_attn_Wq': 6.525, 'L0_attn_Wk': 3.951}
    for name, (base, spread) in spreads.items():
        noise = np.random.default_rng([zlib.crc32(name.encode()), seed]).standard_normal(out[name].shape)
        drawn = base * np.exp(spread * noise) if base else spread * noise
        out[name] = jnp.asarray(drawn.astype(out[name].dtype))
    for name, factor in factors.items():
        out[name] = (out[name] * factor).astype(out[name].dtype)
    return out
```

```python
from contextlib import ExitStack

import concourse.bass as bass
from concourse import mybir

F32 = mybir.dt.float32
F32R = mybir.dt.float32r
ALU = mybir.AluOpType
ACT = mybir.ActivationFunctionType
AX_X = mybir.AxisListType.X
ds = bass.ds

P = 128
C_IDENT, C_RANK, C_HI, C_LO, C_HALF, C_END = 0, 128, 256, 260, 264, 266

CHUNKS = [("K", 0), ("V", 0), ("Q", 0), ("K", 1), ("V", 1), ("Q", 1), ("K", 2), ("V", 2), ("Q", 2),
          ("Q", 3), ("K", 3), ("V", 3)]
NCH = len(CHUNKS)
KQ = [c for c in CHUNKS if c[0] != "V"]
NKQ = len(KQ)


def build(nc, x, xT, wkT, wvT, wqT, woT, gateT, expert_w, expert_b, consts, out):
    C = x.shape[-1]
    NT = x.shape[0] // P
    NB = 4
    TPB = NT // NB
    KC = C // P
    NH, DH = 16, 32
    HG = P // DH
    E = gateT.shape[-1]
    GW = P + 2
    OW = P + HG
    assert (KC, NT, TPB, E) == (4, 16, 4, 8)
    WK, WV, WQ, WO = range(4)
    EPS = 1e-5

    with ExitStack() as ctx:
        def sb(name, shape, dt=F32):
            return ctx.enter_context(nc.sbuf_tensor(name, shape, dt))

        def sem(name):
            return ctx.enter_context(nc.semaphore(name))

        acc = sb("acc", [P, NT, C])
        big_hi = sb("big_hi", [P, 4 * KC, C], F32R)
        big_lo = sb("big_lo", [P, 4 * KC, C], F32R)
        x_raw = sb("x_raw", [P, TPB, KC, P])
        xT_hi = sb("xT_hi", [P, KC, TPB * P], F32R)
        xT_lo = sb("xT_lo", [P, KC, TPB * P], F32R)
        bias_bd = xT_hi
        w_raw = sb("w_raw", [P, KC, C])
        k_sb = sb("k_sb", [P, 2, C])
        v_sb = sb("v_sb", [P, 2, KC, GW])
        exp_sb = sb("exp_sb", [P, 2, C])
        q_new = sb("q_new", [P, KC, TPB * P])
        q_cur = sb("q_cur", [P, KC, TPB * P])
        kvbd = sb("kvbd", [P, KC, OW])
        attn = sb("attn", [P, C])
        attnT_hi = sb("attnT_hi", [P, KC, P], F32R)
        attnT_lo = sb("attnT_lo", [P, KC, P], F32R)
        ew_hi = sb("ew_hi", [P, 2, KC, C], F32R)
        ew_lo = sb("ew_lo", [P, 2, KC, C], F32R)
        gate_raw = sb("gate_raw", [P, KC, E])
        gate_hl = sb("gate_hl", [P, KC, 2 * E], F32R)
        cst = sb("cst", [P, C_END])
        den = sb("den", [P, NH])
        zden = sb("zden", [P, NH])
        stats = sb("stats", [P, 6])
        mv = sb("mv", [P, 2])
        var_eps = sb("var_eps", [P, 1])
        rstd = sb("rstd", [P, 1])
        nbias = sb("nbias", [P, 1])
        idle = sb("idle", [P, 1])
        logit = sb("logit", [P, NT, E])
        work = sb("work", [P, NT, E])
        one1 = sb("one1", [P, NT, E])
        one2 = sb("one2", [P, NT, E])
        gates = sb("gates", [P, NT, E])
        top1 = sb("top1", [P, NT])
        top2 = sb("top2", [P, NT])
        pick = sb("pick", [P, NT])
        g1 = sb("g1", [P, NT])
        g2 = sb("g2", [P, NT])
        gate4 = sb("gate4", [P, NT, 4 * E], F32R)
        gT = sb("gT", [P, NT // 4, P], F32R)
        ident = cst[:, C_IDENT:C_IDENT + P]
        rank = cst[:, C_RANK:C_RANK + NT * E].rearrange("p (t e) -> p t e", e=E)
        minus_half = cst[:, C_HALF:C_HALF + 1]
        bias_raw, bias_lo = k_sb[:, 0, :], k_sb[:, 1, :]
        bias_hi = attnT_hi[:, :, :].rearrange("p k t -> p (k t)")
        yout = exp_sb

        ps = ctx.enter_context(nc.psum_tensor("ps", [P, 8, C], F32))
        B_WO, B_KV, B_OUT, B_TR = 2, 3, 5, 7
        B_LOG, B_XT = 5, 6
        kv_ps = ps[:, B_KV:B_KV + 2, 0:2 * GW].rearrange("p b (g n) -> p b g n", g=2)
        out_ps = ps[:, B_OUT:B_OUT + 2, 0:2 * OW].rearrange("p b (g n) -> p b g n", g=2)
        kvbd_v = kvbd[:, :, :].rearrange("p (b g) n -> p b g n", g=2)

        cst_in, gate_in, x_in, bias_in = sem("cst_in"), sem("gate_in"), sem("x_in"), sem("bias_in")
        w_in = [sem(f"w{n}_in") for n in "kvqo"]
        xT_in = [sem(f"xT{i}_in") for i in range(TPB)]
        ew_in = sem("ew_in")
        stored = [sem("stored0"), sem("stored1")]
        zeroed = sem("zeroed")
        xT_hi_ready, xT_ready = sem("xT_hi_ready"), sem("xT_ready")
        w_hi_ready, w_ready = sem("w_hi_ready"), sem("w_ready")
        ew_hi_ready, ew_ready = sem("ew_hi_ready"), sem("ew_ready")
        gate_hi_ready, gate_ready = sem("gate_hi_ready"), sem("gate_ready")
        proj_done, exp_done, kq_taken, kq_ready = sem("proj_done"), sem("exp_done"), sem("kq_taken"), sem("kq_ready")
        v_ready, kv_done, kvbd_ready, q_moved = sem("v_ready"), sem("kv_done"), sem("kvbd_ready"), sem("q_moved")
        out_done, den_ready, z_ready, attn_ready = sem("out_done"), sem("den_ready"), sem("z_ready"), sem("attn_ready")
        tr_done, attnT_hi_ready, attnT_ready = sem("tr_done"), sem("attnT_hi_ready"), sem("attnT_ready")
        wo_done, h_ready = sem("wo_done"), sem("h_ready")
        stats_ready, mv_ready, var_ready = sem("stats_ready"), sem("mv_ready"), sem("var_ready")
        rstd_ready, norm_ready, x1_ready = sem("rstd_ready"), sem("norm_ready"), sem("x1_ready")
        x1tr_done, x1T_hi_ready, x1T_ready = sem("x1tr_done"), sem("x1T_hi_ready"), sem("x1T_ready")
        logits_done, logits_read, gstep, diff_ready = sem("logits_done"), sem("logits_read"), sem("gstep"), sem("diff_ready")
        expd_ready, gates_ready, gtr_done, gT_ready = sem("expd_ready"), sem("gates_ready"), sem("gtr_done"), sem("gT_ready")
        y_done, y_used, bias_done, bias_used = sem("y_done"), sem("y_used"), sem("bias_done"), sem("bias_used")
        bias_hi_ready, bias_lo_ready, bstep = sem("bias_hi_ready"), sem("bias_lo_ready"), sem("bstep")
        y_out = sem("y_out")

        ew_src = expert_w.rearrange("e (k p) o -> e p k o", p=P)

        block = ctx.enter_context(nc.Block())

        @block.sync
        def _(sp):
            def load_xT(i, tile):
                sp.dma_start(x_raw[:, i, :, :], xT[tile].rearrange("p (k t) -> p k t", k=KC)).then_inc(xT_in[i], 16)

            load_xT(0, 0)
            for k in range(KC):
                sp.dma_start(w_raw[:, k, :], wkT[:, k, :]).then_inc(w_in[WK], 16)
            sp.dma_start(q_cur[:, :, :], wvT).then_inc(w_in[WV], 16)
            sp.dma_start(q_new[:, :, :], wqT).then_inc(w_in[WQ], 16)
            for i in range(1, TPB):
                load_xT(i, i)
            sp.wait_ge(w_ready, 1)
            sp.dma_start(w_raw[:, :, :], woT).then_inc(w_in[WO], 16)
            sp.dma_start(acc[:, :, :], x.rearrange("(t p) c -> p t c", p=P)).then_inc(x_in, 16)
            sp.wait_ge(w_ready, 4)
            sp.dma_start(w_raw[:, :, :], ew_src[0]).then_inc(ew_in, 16)
            with sp.Fori(1, NB) as b:
                for i in range(TPB):
                    sp.wait_ge(xT_ready, TPB * b - TPB + i + 1)
                    sp.dma_start(x_raw[:, i, :, :],
                                 xT[ds(TPB * b + i, 1)].rearrange("a p (k t) -> (a p) k t", k=KC))\
                        .then_inc(xT_in[i], 16)
            sp.wait_ge(kv_done, NT)
            for r in range(P // E):
                sp.dma_start(bias_raw[r * E:(r + 1) * E, :], expert_b).then_inc(bias_in, 16)
            with sp.Fori(1, E) as e:
                sp.wait_ge(ew_ready, e)
                sp.dma_start(w_raw[:, :, :], ew_src[ds(e, 1)].rearrange("a p k o -> (a p) k o")).then_inc(ew_in, 16)
            for t in range(NT):
                sp.wait_ge(y_out, t + 1)
                sp.dma_start(out[t * P:(t + 1) * P, :], yout[:, t % 2, :]).then_inc(stored[t % 2], 16)
            for s in stored:
                sp.wait_ge(s, 16 * (NT // 2))

        def is_first(b):
            return isinstance(b, int) and b == 0

        def kq_number(kind, i):
            return KQ.index((kind, i)) + 1

        @block.gpsimd
        def _(pool):
            pool.dma_start(cst[:, :], consts).then_inc(cst_in, 16)
            pool.dma_start(gate_raw[:, :, :], gateT).then_inc(gate_in, 16)
            nc.gpsimd.memset(kvbd[:, :, :], 0.0).then_inc(zeroed, 1)
            nc.gpsimd.memset(v_sb[:, :, :, :], 1.0).then_inc(zeroed, 1)

            def power(n):
                pool.wait_ge(var_ready, n + 1)
                nc.gpsimd.tensor_tensor(rstd[:, :], var_eps[:, :], minus_half, ALU.pow).then_inc(rstd_ready, 1)

            def split_expert(e, buf):
                pool.wait_ge(ew_hi_ready, e + 1)
                nc.gpsimd.tensor_tensor(ew_lo[:, buf], w_raw[:, :, :], ew_hi[:, buf].bitcast(F32),
                                        ALU.subtract).then_inc(ew_ready, 1)

            pool.wait_ge(cst_in, 16)
            with pool.Fori(1, NB) as b:
                power(TPB * b - TPB)
                power(TPB * b - TPB + 1)
                power(TPB * b - TPB + 2)
                power(TPB * b - TPB + 3)
            split_expert(0, 0)
            for i in range(TPB):
                power(NT - TPB + i)
            split_expert(1, 1)
            with pool.Fori(1, E // 2) as j:
                split_expert(2 * j, 0)
                split_expert(2 * j + 1, 1)
            for t in range(NT):
                power(NT + t)

        @block.scalar
        def _(act):
            def split_x(b, i):
                tok = slice(i * P, (i + 1) * P)
                act.wait_ge(xT_in[i], 16 * b + 16)
                if not is_first(b):
                    act.wait_ge(proj_done, NCH * b - (2 if i < 3 else 0))
                nc.scalar.copy(xT_hi[:, :, tok], x_raw[:, i, :, :]).then_inc(xT_hi_ready, 1)

            def split_w(m, raw):
                act.wait_ge(w_in[m], 64 if m == WK else 16)
                nc.scalar.copy(big_hi[:, m * KC:(m + 1) * KC, :], raw[:, :, :]).then_inc(w_hi_ready, 1)

            def split_expert(e, buf):
                act.wait_ge(ew_in, 16 * e + 16)
                if not isinstance(e, int) or e >= 2:
                    act.wait_ge(y_done, NT * e - NT)
                nc.scalar.copy(ew_hi[:, buf], w_raw[:, :, :]).then_inc(ew_hi_ready, 1)

            def exp_of(b, kind, i):
                at, n = CHUNKS.index((kind, i)), kq_number(kind, i)
                act.wait_ge(proj_done, NCH * b + at + 1)
                if n > 2 or not is_first(b):
                    act.wait_ge(kq_ready, NKQ * b + n - 2)
                nc.scalar.activation(exp_sb[:, n % 2, :], ps[:, at % 2, :], ACT.Exp).then_inc(exp_done, 1)

            def take_v(b, i):
                at = CHUNKS.index(("V", i))
                act.wait_ge(proj_done, NCH * b + at + 1)
                if i >= 2 or not is_first(b):
                    act.wait_ge(kv_done, TPB * b + i - 1)
                else:
                    act.wait_ge(zeroed, 2)
                nc.scalar.copy(v_sb[:, i % 2, :, 0:P],
                               ps[:, at % 2, :].rearrange("p (g n) -> p g n", g=KC)).then_inc(v_ready, 1)

            def attnT_high(m):
                act.wait_ge(tr_done, m + 1)
                nc.scalar.copy(attnT_hi[:, :, :], ps[:, B_TR, :].rearrange("p (k t) -> p k t", k=KC))\
                    .then_inc(attnT_hi_ready, 1)

            def normalise_x1(m):
                act.wait_ge(norm_ready, m + 1)
                a = acc[:, ds(m, 1), :]
                nc.scalar.activation(a, a, ACT.Identity, bias=nbias[:, :], scale=rstd[:, :]).then_inc(x1_ready, 1)

            def move_q(b):
                act.wait_ge(kq_ready, NKQ * b + kq_number("Q", 3))
                for i in range(TPB):
                    tok = slice(i * P, (i + 1) * P)
                    if not is_first(b):
                        act.wait_ge(out_done, TPB * b - TPB + i + 1)
                    nc.scalar.copy(q_cur[:, :, tok], q_new[:, :, tok]).then_inc(q_moved, 1)

            split_x(0, 0)
            split_w(WK, w_raw)
            split_w(WV, q_cur)
            for i in range(1, TPB):
                split_x(0, i)
            split_w(WQ, q_new)
            act.wait_ge(gate_in, 16)
            nc.scalar.copy(gate_hl[:, :, 0:E], gate_raw[:, :, :]).then_inc(gate_hi_ready, 1)
            for kind, i in CHUNKS[:-1]:
                if kind == "V":
                    take_v(0, i)
                else:
                    exp_of(0, kind, i)
                if (kind, i) == ("Q", 1):
                    split_w(WO, w_raw)
            move_q(0)
            with act.Fori(1, NB) as b:
                m = TPB * b - TPB
                split_x(b, 0)
                take_v(b - 1, 3)
                split_x(b, 1)
                split_x(b, 2)
                split_x(b, 3)
                exp_of(b, "K", 0)
                take_v(b, 0)
                exp_of(b, "Q", 0)
                attnT_high(m)
                exp_of(b, "K", 1)
                take_v(b, 1)
                normalise_x1(m)
                exp_of(b, "Q", 1)
                attnT_high(m + 1)
                exp_of(b, "K", 2)
                take_v(b, 2)
                normalise_x1(m + 1)
                exp_of(b, "Q", 2)
                attnT_high(m + 2)
                exp_of(b, "Q", 3)
                attnT_high(m + 3)
                normalise_x1(m + 2)
                exp_of(b, "K", 3)
                normalise_x1(m + 3)
                move_q(b)
            m = NT - TPB
            take_v(NB - 1, 3)
            split_expert(0, 0)
            attnT_high(m)
            attnT_high(m + 1)
            normalise_x1(m)
            attnT_high(m + 2)
            normalise_x1(m + 1)
            attnT_high(m + 3)
            normalise_x1(m + 2)
            normalise_x1(m + 3)
            act.wait_ge(proj_done, NCH * NB)
            act.wait_ge(wo_done, NT)
            for t in range(NT):
                act.wait_ge(x1tr_done, t + 1)
                nc.scalar.copy(big_hi[:, t, :], ps[:, B_XT + t % 2, :]).then_inc(x1T_hi_ready, 1)
            act.wait_ge(bias_in, 16 * (P // E))
            nc.scalar.copy(bias_hi, bias_raw).then_inc(bias_hi_ready, 1)
            act.wait_ge(diff_ready, 1)
            nc.scalar.activation(g2[:, :], pick[:, :], ACT.Exp).then_inc(expd_ready, 1)
            act.wait_ge(gtr_done, 1)
            nc.scalar.copy(gT[:, :, :], ps[:, B_LOG, :].rearrange("p (q t) -> p q t", q=NT // 4)).then_inc(gT_ready, 1)
            split_expert(1, 1)
            with act.Fori(1, E // 2) as j:
                split_expert(2 * j, 0)
                split_expert(2 * j + 1, 1)
            for t in range(NT):
                act.wait_ge(norm_ready, NT + t + 1)
                if t >= 2:
                    act.wait_ge(stored[t % 2], 16 * (t // 2))
                nc.scalar.activation(yout[:, t % 2, :], acc[:, t, :], ACT.Identity, bias=nbias[:, :],
                                     scale=rstd[:, :]).then_inc(y_out, 1)

        @block.vector
        def _(dve):
            def split_x(b, i):
                tok = slice(i * P, (i + 1) * P)
                dve.wait_ge(xT_hi_ready, TPB * b + i + 1)
                nc.vector.tensor_tensor(xT_lo[:, :, tok], x_raw[:, i, :, :], xT_hi[:, :, tok].bitcast(F32),
                                        ALU.subtract).then_inc(xT_ready, 1)

            def split_w(m, raw):
                at = slice(m * KC, (m + 1) * KC)
                dve.wait_ge(w_hi_ready, m + 1)
                nc.vector.tensor_tensor(big_lo[:, at, :], raw[:, :, :], big_hi[:, at, :].bitcast(F32),
                                        ALU.subtract).then_inc(w_ready, 1)

            def feature_map(b, kind, i):
                at, n = CHUNKS.index((kind, i)), kq_number(kind, i)
                if kind == "K":
                    dst = k_sb[:, i % 2, :]
                    if not is_first(b) or i >= 2:
                        dve.wait_ge(kv_done, TPB * b + i - 1)
                else:
                    dst = q_new[:, i, :]
                    if not is_first(b):
                        dve.wait_ge(q_moved, TPB * b)
                dve.wait_ge(exp_done, NKQ * b + n)
                nc.vector.tensor_scalar(dst, ps[:, at % 2, :], 0.0, None, ALU.max).then_inc(kq_taken, 1)
                dve.wait_ge(kq_taken, NKQ * b + n)
                nc.vector.scalar_tensor_tensor(out=dst, in0=exp_sb[:, n % 2, :], scalar=1.0, in1=dst,
                                               op0=ALU.min, op1=ALU.add).then_inc(kq_ready, 1)

            def take_kv(b):
                dve.wait_ge(kv_done, TPB * b + TPB)
                dve.wait_ge(zeroed, 2)
                for j in range(HG):
                    h = slice(j * DH, (j + 1) * DH)
                    nc.vector.tensor_copy(kvbd_v[h, :, :, h], kv_ps[h, :, :, h]).then_inc(kvbd_ready, 1)
                    nc.vector.tensor_copy(kvbd_v[h, :, :, P + j:P + j + 1], kv_ps[h, :, :, P:P + 1])\
                        .then_inc(kvbd_ready, 1)

            def take_out(m):
                dve.wait_ge(out_done, m + 1)
                nc.vector.tensor_scalar(den[:, :].rearrange("p (b g h) -> p b g h", b=2, g=2),
                                        out_ps[:, :, :, P:OW], 1e-6, None, ALU.add).then_inc(den_ready, 1)
                dve.wait_ge(den_ready, m + 1)
                nc.vector.reciprocal(zden[:, :], den[:, :]).then_inc(z_ready, 1)
                dve.wait_ge(z_ready, m + 1)
                for c in range(2):
                    half = slice(c * 2 * P, (c + 1) * 2 * P)
                    nc.vector.tensor_tensor(
                        attn[:, half].rearrange("p (g h e) -> p g h e", g=2, h=HG),
                        out_ps[:, c, :, 0:P].rearrange("p g (h e) -> p g h e", h=HG),
                        zden[:, c * 8:c * 8 + 8].rearrange("p (g h) -> p g h", g=2).unsqueeze(3)
                        .to_broadcast([P, 2, HG, DH]), ALU.mult).then_inc(attn_ready, 1)

            def attnT_low(m):
                dve.wait_ge(attnT_hi_ready, m + 1)
                nc.vector.tensor_tensor(attnT_lo[:, :, :], ps[:, B_TR, :].rearrange("p (k t) -> p k t", k=KC),
                                        attnT_hi[:, :, :].bitcast(F32), ALU.subtract).then_inc(attnT_ready, 1)

            def carry_wait():
                nc.vector.tensor_copy(idle[:, :], minus_half)

            def norm_terms(n, a, taken=None, before=0):
                nc.vector.bn_stats(stats[:, :], a).then_inc(stats_ready, 1)
                dve.wait_ge(stats_ready, n + 1)
                carry_wait()
                nc.vector.bn_aggr(mv[:, :], stats[:, :]).then_inc(mv_ready, 1)
                dve.wait_ge(mv_ready, n + 1)
                if taken is not None:
                    dve.wait_ge(taken, before)
                nc.vector.tensor_scalar(var_eps[:, :], mv[:, 1:2], EPS, None, ALU.add).then_inc(var_ready, 1)
                dve.wait_ge(rstd_ready, n + 1)
                nc.vector.tensor_scalar(nbias[:, :], mv[:, 0:1], rstd[:, 0:1], -1.0, ALU.mult, ALU.mult)\
                    .then_inc(norm_ready, 1)

            def take_wo(m, i):
                m = m + i
                dve.wait_ge(wo_done, m + 1)
                a = acc[:, ds(m, 1), :]
                nc.vector.tensor_tensor(a, ps[:, B_WO:B_WO + 1, :], a, ALU.add).then_inc(h_ready, 1)
                dve.wait_ge(h_ready, m + 1)
                carry_wait()
                if i > 0:
                    norm_terms(m, a, x1_ready, m)
                else:
                    norm_terms(m, a)

            split_x(0, 0)
            split_w(WK, w_raw)
            split_w(WV, q_cur)
            for i in range(1, TPB):
                split_x(0, i)
            split_w(WQ, q_new)
            dve.wait_ge(gate_hi_ready, 1)
            nc.vector.tensor_tensor(gate_hl[:, :, E:2 * E], gate_raw[:, :, :], gate_hl[:, :, 0:E].bitcast(F32),
                                    ALU.subtract).then_inc(gate_ready, 1)
            for kind, i in KQ:
                feature_map(0, kind, i)
                if (kind, i) == ("Q", 1):
                    split_w(WO, w_raw)
            dve.wait_ge(x_in, 16)
            with dve.Fori(1, NB) as b:
                m = TPB * b - TPB
                for i in range(TPB):
                    split_x(b, i)
                feature_map(b, "K", 0)
                take_kv(b - 1)
                take_out(m)
                feature_map(b, "Q", 0)
                attnT_low(m)
                feature_map(b, "K", 1)
                take_wo(m, 0)
                take_out(m + 1)
                feature_map(b, "Q", 1)
                attnT_low(m + 1)
                feature_map(b, "K", 2)
                take_wo(m, 1)
                take_out(m + 2)
                feature_map(b, "Q", 2)
                attnT_low(m + 2)
                take_out(m + 3)
                feature_map(b, "Q", 3)
                attnT_low(m + 3)
                take_wo(m, 2)
                feature_map(b, "K", 3)
                take_wo(m, 3)
            m = NT - TPB
            take_kv(NB - 1)
            take_out(m)
            attnT_low(m)
            take_out(m + 1)
            take_wo(m, 0)
            attnT_low(m + 1)
            take_out(m + 2)
            take_wo(m, 1)
            attnT_low(m + 2)
            take_out(m + 3)
            take_wo(m, 2)
            attnT_low(m + 3)
            take_wo(m, 3)
            for t in range(NT):
                dve.wait_ge(x1T_hi_ready, t + 1)
                nc.vector.tensor_tensor(big_lo[:, t, :], ps[:, B_XT + t % 2, :], big_hi[:, t, :].bitcast(F32),
                                        ALU.subtract).then_inc(x1T_ready, 1)

            steps = [0]

            def link(ins):
                steps[0] += 1
                ins.then_inc(gstep, 1)
                dve.wait_ge(gstep, steps[0])

            def over_experts(a):
                return a[:, :].unsqueeze(2).to_broadcast([P, NT, E])

            def argmax(one, top):
                link(nc.vector.tensor_reduce(top[:, :], work[:, :, :], AX_X, ALU.max))
                link(nc.vector.tensor_tensor(one[:, :, :], work[:, :, :], over_experts(top), ALU.is_equal))
                link(nc.vector.tensor_tensor(one[:, :, :], one[:, :, :], rank, ALU.mult))
                link(nc.vector.tensor_reduce(pick[:, :], one[:, :, :], AX_X, ALU.max))
                link(nc.vector.tensor_tensor(one[:, :, :], one[:, :, :], over_experts(pick), ALU.is_equal))

            dve.wait_ge(logits_done, NT)
            nc.vector.tensor_reduce(logit[:, :, :], ps[:, B_LOG, 0:NT * 2 * E].rearrange(
                "p (t a e) -> p t e a", a=2, e=E), AX_X, ALU.add).then_inc(logits_read, 1)
            dve.wait_ge(logits_read, 1)
            link(nc.vector.tensor_copy(work[:, :, :], logit[:, :, :]))
            argmax(one1, top1)
            link(nc.vector.tensor_scalar(work[:, :, :], one1[:, :, :], -3.0e38, None, ALU.mult))
            link(nc.vector.tensor_tensor(work[:, :, :], work[:, :, :], logit[:, :, :], ALU.add))
            argmax(one2, top2)
            nc.vector.tensor_tensor(pick[:, :], top2[:, :], top1[:, :], ALU.subtract).then_inc(diff_ready, 1)
            dve.wait_ge(expd_ready, 1)
            link(nc.vector.tensor_scalar(g1[:, :], g2[:, :], 1.0, None, ALU.add))
            link(nc.vector.reciprocal(g1[:, :], g1[:, :]))
            link(nc.vector.tensor_tensor(g2[:, :], g2[:, :], g1[:, :], ALU.mult))
            link(nc.vector.tensor_tensor(one1[:, :, :], one1[:, :, :], over_experts(g1), ALU.mult))
            link(nc.vector.tensor_tensor(one2[:, :, :], one2[:, :, :], over_experts(g2), ALU.mult))
            link(nc.vector.tensor_tensor(gates[:, :, :], one1[:, :, :], one2[:, :, :], ALU.add))
            link(nc.vector.tensor_copy(gate4[:, :, 0:E], gates[:, :, :]))
            nc.vector.tensor_copy(gate4[:, :, E:2 * E], gates[:, :, :]).then_inc(gates_ready, 1)
            for q in (2, 3):
                nc.vector.tensor_tensor(gate4[:, :, q * E:(q + 1) * E], gates[:, :, :],
                                        gate4[:, :, 0:E].bitcast(F32), ALU.subtract).then_inc(gates_ready, 1)

            def add_expert(e, t, bank):
                dve.wait_ge(y_done, NT * e + t + 1)
                gate = gates[:, t, e:e + 1] if isinstance(e, int) else gates[:, t, ds(e, 1)]
                nc.vector.scalar_tensor_tensor(out=acc[:, t, :], in0=ps[:, bank, :], scalar=gate,
                                               in1=acc[:, t, :], op0=ALU.mult, op1=ALU.add).then_inc(y_used, 1)

            for t in range(NT):
                add_expert(0, t, t % 8)
            dve.wait_ge(bias_hi_ready, 1)
            nc.vector.tensor_tensor(bias_lo, bias_raw, bias_hi.bitcast(F32), ALU.subtract).then_inc(bstep, 1)
            dve.wait_ge(bstep, 1)
            for j in range(4):
                nc.vector.tensor_scalar(bias_bd[:, j, :], bias_lo, cst[:, C_LO + j:C_LO + j + 1], None, ALU.mult)\
                    .then_inc(bstep, 1)
                dve.wait_ge(bstep, 2 + 2 * j)
                nc.vector.scalar_tensor_tensor(out=bias_bd[:, j, :], in0=bias_hi.bitcast(F32),
                                               scalar=cst[:, C_HI + j:C_HI + j + 1],
                                               in1=bias_bd[:, j, :].bitcast(F32), op0=ALU.mult, op1=ALU.add)\
                    .then_inc(bstep, 1)
            with dve.Fori(1, E - 1) as e:
                for t in range(NT):
                    dve.wait_ge(y_used, NT * e + t)
                    add_expert(e, t, t % 8)
            for t in range(NT):
                add_expert(E - 1, t, t % 4)
                dve.wait_ge(bias_done, t + 1)
                dve.wait_ge(y_used, NT * (E - 1) + t + 1)
                nc.vector.tensor_tensor(acc[:, t, :], ps[:, 4 + t % 4, :], acc[:, t, :], ALU.add).then_inc(bias_used, 1)
                dve.wait_ge(bias_used, t + 1)
                norm_terms(NT + t, acc[:, t, :], *((y_out, t) if t else ()))

        @block.tensor
        def _(pe):
            def three(bank, lhs_hi, lhs_lo, rhs_hi, rhs_lo):
                for k in range(KC):
                    nc.tensor.matmul(bank, lhs_hi(k), rhs_hi(k), start=(k == 0), stop=False)
                    nc.tensor.matmul(bank, lhs_hi(k), rhs_lo(k), start=False, stop=False)
                    last = nc.tensor.matmul(bank, lhs_lo(k), rhs_hi(k), start=False, stop=(k == KC - 1))
                return last

            def project(b, kind, i):
                at = CHUNKS.index((kind, i))
                if is_first(b):
                    pe.wait_ge(w_ready, {"K": 1, "V": 2, "Q": 3}[kind])
                pe.wait_ge(xT_ready, TPB * b + (TPB if kind == "Q" else i + 1))
                if not is_first(b) or at >= 2:
                    back, bb = CHUNKS[(at - 2) % NCH], b - (at < 2)
                    if back[0] == "V":
                        pe.wait_ge(v_ready, TPB * bb + back[1] + 1)
                    else:
                        pe.wait_ge(kq_taken, NKQ * bb + kq_number(*back))
                bank = ps[:, at % 2, :]
                if kind == "Q":
                    col = slice(i * P, (i + 1) * P)
                    last = three(bank, lambda k: big_hi[:, WQ * KC + k, col], lambda k: big_lo[:, WQ * KC + k, col],
                                 lambda k: xT_hi[:, k, :], lambda k: xT_lo[:, k, :])
                else:
                    tok, w = slice(i * P, (i + 1) * P), (WK if kind == "K" else WV) * KC
                    last = three(bank, lambda k: xT_hi[:, k, tok], lambda k: xT_lo[:, k, tok],
                                 lambda k: big_hi[:, w + k, :], lambda k: big_lo[:, w + k, :])
                last.then_inc(proj_done, 1)

            def kv(b, i):
                pe.wait_ge(kq_ready, NKQ * b + kq_number("K", i))
                pe.wait_ge(v_ready, TPB * b + i + 1)
                if i == 0 and not is_first(b):
                    pe.wait_ge(kvbd_ready, 2 * HG * b)
                for g in range(KC):
                    last = nc.tensor.matmul(kv_ps[:, g // 2, g % 2, :], k_sb[:, i % 2, g * P:(g + 1) * P],
                                            v_sb[:, i % 2, g, :], start=(i == 0 and g % 2 == 0), stop=(i == TPB - 1),
                                            skip_group_check=True)
                last.then_inc(kv_done, 1)

            def attend(b, m, i):
                pe.wait_ge(q_moved, m + 1)
                pe.wait_ge(kvbd_ready, 2 * HG * b + 2 * HG)
                for g in range(KC):
                    last = nc.tensor.matmul(out_ps[:, g // 2, g % 2, :], q_cur[:, g, i * P:(i + 1) * P],
                                            kvbd[:, g, :], start=True, stop=True)
                last.then_inc(out_done, 1)

            def turn(m):
                pe.wait_ge(attn_ready, 2 * m + 2)
                for k in range(KC):
                    last = nc.tensor.transpose(ps[:, B_TR, k * P:(k + 1) * P], attn[:, k * P:(k + 1) * P], ident)
                last.then_inc(tr_done, 1)

            def output(m, i):
                m = m + i
                pe.wait_ge(attnT_ready, m + 1)
                if i > 0:
                    pe.wait_ge(h_ready, m)
                three(ps[:, B_WO, :], lambda k: attnT_hi[:, k, :], lambda k: attnT_lo[:, k, :],
                      lambda k: big_hi[:, WO * KC + k, :], lambda k: big_lo[:, WO * KC + k, :]).then_inc(wo_done, 1)

            project(0, "K", 0)
            project(0, "V", 0)
            project(0, "Q", 0)
            project(0, "K", 1)
            kv(0, 0)
            project(0, "V", 1)
            project(0, "Q", 1)
            project(0, "K", 2)
            kv(0, 1)
            project(0, "V", 2)
            project(0, "Q", 2)
            project(0, "Q", 3)
            project(0, "K", 3)
            project(0, "V", 3)
            kv(0, 2)
            pe.wait_ge(w_ready, 4)
            pe.wait_ge(cst_in, 16)
            with pe.Fori(1, NB) as b:
                m = TPB * b - TPB
                project(b, "K", 0)
                kv(b - 1, 3)
                project(b, "V", 0)
                attend(b - 1, m, 0)
                project(b, "Q", 0)
                turn(m)
                project(b, "K", 1)
                output(m, 0)
                kv(b, 0)
                project(b, "V", 1)
                attend(b - 1, m + 1, 1)
                project(b, "Q", 1)
                turn(m + 1)
                project(b, "K", 2)
                output(m, 1)
                kv(b, 1)
                project(b, "V", 2)
                attend(b - 1, m + 2, 2)
                project(b, "Q", 2)
                turn(m + 2)
                attend(b - 1, m + 3, 3)
                project(b, "Q", 3)
                output(m, 2)
                turn(m + 3)
                project(b, "K", 3)
                output(m, 3)
                project(b, "V", 3)
                kv(b, 2)
            m = NT - TPB
            kv(NB - 1, 3)
            attend(NB - 1, m, 0)
            turn(m)
            for i in range(1, TPB):
                attend(NB - 1, m + i, i)
                output(m, i - 1)
                turn(m + i)
            output(m, TPB - 1)

            def turn_x1(t):
                pe.wait_ge(x1_ready, t + 1)
                if t >= 2:
                    pe.wait_ge(x1T_ready, t - 1)
                for k in range(KC):
                    last = nc.tensor.transpose(ps[:, B_XT + t % 2, k * P:(k + 1) * P],
                                               acc[:, t, k * P:(k + 1) * P], ident)
                last.then_inc(x1tr_done, 1)

            def logits(t):
                pe.wait_ge(x1T_ready, t + 1)
                to = ps[:, B_LOG, t * 2 * E:(t + 1) * 2 * E]
                for k in range(KC):
                    tok = slice(k * P, (k + 1) * P)
                    nc.tensor.matmul(to, big_hi[:, t, tok], gate_hl[:, k, :], start=(k == 0), stop=False)
                    last = nc.tensor.matmul(to, big_lo[:, t, tok], gate_hl[:, k, :], start=False, stop=(k == KC - 1))
                last.then_inc(logits_done, 1)

            def expert(buf, t, bank):
                three(ps[:, bank, :], lambda k: big_hi[:, t, k * P:(k + 1) * P],
                      lambda k: big_lo[:, t, k * P:(k + 1) * P],
                      lambda k: ew_hi[:, buf, k, :], lambda k: ew_lo[:, buf, k, :]).then_inc(y_done, 1)

            early = B_LOG
            pe.wait_ge(gate_ready, 1)
            for t in range(NT + 1):
                if t < NT:
                    turn_x1(t)
                if t >= 1:
                    logits(t - 1)
                if t == 1:
                    pe.wait_ge(ew_ready, 1)
                    pe.wait_ge(h_ready, NT)
                    pe.wait_ge(kvbd_ready, 2 * HG * NB)
                    pe.wait_ge(kq_taken, NKQ * NB)
                    pe.wait_ge(v_ready, NT)
                if 1 <= t <= early:
                    expert(0, t - 1, t - 1)
            pe.wait_ge(gates_ready, 3)
            for q in range(NT // 4):
                last = nc.tensor.transpose(ps[:, B_LOG, q * P:(q + 1) * P],
                                           gate4[:, 4 * q:4 * q + 4, :].rearrange("p t r -> p (t r)").bitcast(F32),
                                           ident)
            last.then_inc(gtr_done, 1)
            pe.wait_ge(gT_ready, 1)
            pe.wait_ge(x1T_ready, NT)
            for t in range(early, NT):
                if t >= 8:
                    pe.wait_ge(y_used, t - 7)
                expert(0, t, t % 8)
            with pe.Fori(0, (E - 2) // 2) as j:
                for one in (1, 2):
                    pe.wait_ge(ew_ready, 2 * j + one + 1)
                    for t in range(NT):
                        pe.wait_ge(y_used, NT * (2 * j + one) + t - 7)
                        expert(one % 2, t, t % 8)
            done = NT * (E - 1)
            pe.wait_ge(ew_ready, E)
            pe.wait_ge(bstep, 9)
            for t in range(NT):
                pe.wait_ge(y_used, done - NT + 8 + t + 1 if t < 4 else done + t - 3)
                expert(1, t, t % 4)
                if t < 4:
                    pe.wait_ge(y_used, done - NT + 12 + t + 1)
                else:
                    pe.wait_ge(bias_used, t - 3)
                nc.tensor.matmul(ps[:, 4 + t % 4, :], gT[:, t // 4, :], bias_bd[:, t % 4, :],
                                 start=True, stop=True).then_inc(bias_done, 1)


_INS = ["x", "xT", "wkT", "wvT", "wqT", "woT", "gateT", "expert_w", "expert_b", "consts"]


def kernel(L0_attn_x, L0_attn_cos, L0_attn_sin, L0_attn_Wq, L0_attn_Wk, L0_attn_Wv, L0_attn_Wo,
           L0_ffn_gate_w, L0_ffn_expert_w, L0_ffn_expert_b):
    import numpy as np
    import concourse.bacc as bacc
    from concourse.bass_utils import run_bass_kernel_spmd

    x = np.asarray(L0_attn_x)
    B, T, C = x.shape
    rows = np.ascontiguousarray(x.reshape(B * T, C))

    def by_block(w):
        w = np.asarray(w)
        return np.ascontiguousarray(w.reshape(w.shape[0], C // P, P).transpose(2, 1, 0))

    E = np.asarray(L0_ffn_gate_w).shape[0]
    consts = np.zeros((P, C_END), np.float32)
    consts[:, C_IDENT:C_IDENT + P] = np.eye(P, dtype=np.float32)
    consts[:, C_RANK:C_RANK + P] = np.tile(np.arange(E, 0, -1, dtype=np.float32), P // E)
    part = np.arange(P)
    for j in range(4):
        consts[:, C_HI + j] = (part // 32 == j) & (part // E % 2 == 0)
        consts[:, C_LO + j] = (part // 32 == j) & (part // E % 2 == 1)
    consts[:, C_HALF] = -0.5
    arrays = {
        "x": rows,
        "xT": np.ascontiguousarray(rows.reshape(-1, P, C // P, P).transpose(0, 3, 2, 1)).reshape(-1, P, C),
        "wkT": by_block(L0_attn_Wk), "wvT": by_block(L0_attn_Wv),
        "wqT": by_block(L0_attn_Wq), "woT": by_block(L0_attn_Wo),
        "gateT": by_block(L0_ffn_gate_w),
        "expert_w": np.asarray(L0_ffn_expert_w), "expert_b": np.asarray(L0_ffn_expert_b),
        "consts": consts,
    }
    nc = bacc.Bacc("TRN2", target_bir_lowering=False, num_devices=1)
    args = [nc.dram_tensor(n, arrays[n].shape, F32, kind="ExternalInput").ap() for n in _INS]
    out = nc.dram_tensor("out", rows.shape, F32, kind="ExternalOutput").ap()
    build(nc, *args, out)
    r = run_bass_kernel_spmd(nc, [arrays], core_ids=[0])
    return r.results[0]["out"].reshape(B, T, C)
```

```python
from contextlib import ExitStack

import concourse.bass as bass
from concourse import mybir

F32 = mybir.dt.float32
F32R = mybir.dt.float32r
I32 = mybir.dt.int32
ALU = mybir.AluOpType
ACT = mybir.ActivationFunctionType
AX_X = mybir.AxisListType.X
ds = bass.ds

P = 128
N_EXPERTS, N_TOKENS, TOP = 8, 2048, 2
NS = TOP * N_TOKENS // P + N_EXPERTS - 1
REGION = N_TOKENS
TABLE = N_EXPERTS * REGION + N_EXPERTS * P

_widths = [("IDENT", P), ("TRI", P), ("ONES", P), ("RANK", 4 * N_EXPERTS), ("EBASE", 4 * N_EXPERTS),
           ("BEFORE", N_EXPERTS ** 2), ("SLOT", NS), ("SLOTROW", NS), ("HI", 4), ("LO", 4), ("HALF", 2)]
COL, C_END = {}, 0
for _n, _w in _widths:
    COL[_n] = slice(C_END, C_END + _w)
    C_END += _w

NB, TPB = 4, 4
NT = NB * TPB

CHUNKS = [("K", 0), ("V", 0), ("Q", 0), ("K", 1), ("V", 1), ("Q", 1), ("K", 2), ("V", 2), ("Q", 2),
          ("Q", 3), ("K", 3), ("V", 3)]
NCH = len(CHUNKS)
KQ = [c for c in CHUNKS if c[0] != "V"]
NKQ = len(KQ)


def schedule():
    todo = []
    for b in range(NB):
        c, n = b - 1, b + 1
        after = {
            ("K", 0): [("kv", c, 3)],
            ("V", 0): [("out", c, 0), ("gt", b - 2, 0)],
            ("Q", 0): [("tr", c, 0)],
            ("K", 1): [("wo", c, 0), ("out", c, 1), ("kv", b, 0), ("rt", b - 2, 0)],
            ("V", 1): [("nx", c, 0), ("tr", c, 1)],
            ("Q", 1): [("wo", c, 1), ("out", c, 2), ("xt", c, 0)],
            ("K", 2): [("nx", c, 1), ("tr", c, 2), ("kv", b, 1), ("lg", c, 0)],
            ("V", 2): [("wo", c, 2), ("out", c, 3), ("xt", c, 1)],
            ("Q", 2): [("nx", c, 2), ("tr", c, 3), ("lg", c, 1)],
            ("Q", 3): [("wo", c, 3), ("xt", c, 2), ("x", n, 0)],
            ("K", 3): [("nx", c, 3), ("kv", b, 2), ("lg", c, 2), ("x", n, 1), ("x", n, 2)],
            ("V", 3): [("xt", c, 3), ("x", n, 3), ("lg", c, 3)],
        }
        for chunk in CHUNKS:
            todo.append((chunk[0], b, chunk[1]))
            todo += [s for s in after[chunk] if 0 <= s[1] < NB]
            if b == 0 and chunk == ("Q", 1):
                todo.append(("wo_w", 0, 0))
            if b == 2 and chunk in (("Q", 1), ("Q", 2)):
                todo.append(("we", 0 if chunk[1] == 1 else 1, 0))
    c = NB - 1
    todo += [("kv", c, 3), ("out", c, 0), ("out", c, 1), ("tr", c, 0), ("tr", c, 1), ("wo", c, 0), ("gt", c - 1, 0),
             ("nx", c, 0), ("wo", c, 1), ("out", c, 2), ("rt", c - 1, 0), ("tr", c, 2), ("xt", c, 0), ("nx", c, 1),
             ("wo", c, 2), ("out", c, 3), ("we", 2, 0), ("tr", c, 3), ("lg", c, 0), ("xt", c, 1), ("nx", c, 2),
             ("wo", c, 3), ("lg", c, 1), ("we", 3, 0), ("xt", c, 2), ("nx", c, 3), ("lg", c, 2), ("xt", c, 3), ("lg", c, 3),
             ("gt", c, 0), ("rt", c, 0)]
    return todo


def build(nc, x, xT, wkT, wvT, wqT, woT, gateT, expert_w, expert_b, consts, token_ids, out):
    C = x.shape[-1]
    KC = C // P
    NH, DH = 16, 32
    HG = P // DH
    E = N_EXPERTS
    GW = P + 2
    OW = P + HG
    EPS = 1e-5
    HIP, LOP = 0, 1
    TODO = schedule()
    assert x.shape[0] == N_TOKENS == NT * P and expert_w.shape[0] == E and KC == 4

    x1_rows = nc.dram_tensor("x1_rows", (N_TOKENS, C), F32, kind="Internal").ap()
    y_rows = nc.dram_tensor("y_rows", (NS * P, C), F32, kind="Internal").ap()
    table = nc.dram_tensor("table", (TABLE, 2), I32, kind="Internal").ap()

    with ExitStack() as ctx:
        def sb(name, shape, dt=F32, stack=ctx):
            return stack.enter_context(nc.sbuf_tensor(name, shape, dt))

        def sem(name):
            return ctx.enter_context(nc.semaphore(name))

        acc = sb("acc", [P, NT, C])
        rowT_hi = sb("rowT_hi", [P, 2, KC, P], F32R)
        rowT_lo = sb("rowT_lo", [P, 2, KC, P], F32R)
        gate_raw = sb("gate_raw", [P, KC, E])
        gate_hl = sb("gate_hl", [P, KC, 2 * E], F32R)
        cst = sb("cst", [P, C_END])
        ids = sb("ids", [P, NT], I32)
        stats = sb("stats", [P, 6])
        mv = sb("mv", [P, 2])
        var_eps = sb("var_eps", [P, 1])
        rstd = sb("rstd", [P, 1])
        nbias = sb("nbias", [P, 1])
        logit = sb("logit", [P, TPB, E])
        work = sb("work", [P, NT, E])
        one1 = sb("one1", [P, NT, E])
        one2 = sb("one2", [P, NT, E])
        chosen = sb("chosen", [P, NT, E])
        earlier = sb("earlier", [P, NT + 1, E])
        place = sb("place", [P, NT, E])
        top1 = sb("top1", [P, TPB])
        top2 = sb("top2", [P, TPB])
        pick = sb("pick", [P, NT])
        diff = sb("diff", [P, TPB])
        g1 = sb("g1", [P, TPB])
        g2 = sb("g2", [P, TPB])
        entry = sb("entry", [P, NT, TOP, 2], I32)
        entry_at = sb("entry_at", [P, TOP, NT], I32)
        tiles_i = sb("tiles_i", [P, E], I32)
        tiles = sb("tiles", [P, E])
        first = sb("first", [P, E])
        skip = sb("skip", [P, E])

        with ExitStack() as early:
            sb("experts01", [P, 2, 2, KC, C], F32, early)
            with ExitStack() as raws:
                w_hl = sb("w_hl", [P, 3, 2, KC, C], F32R, raws)
            w_raw = [sb(f"w{n}_raw", [P, 2, KC, C], F32, early) for n in "kvq"]
            xT_hi = sb("xT_hi", [P, KC, TPB * P], F32R, early)
            xT_lo = sb("xT_lo", [P, KC, TPB * P], F32R, early)
            with ExitStack() as raws:
                wo_hl = sb("wo_hl", [P, 2, KC, C], F32R, raws)
            wo_raw = sb("wo_raw", [P, 2, KC, C], F32, early)
            q_sb = sb("q_sb", [P, 2, KC, TPB * P], F32, early)
            x_raw = sb("x_raw", [P, TPB, KC, P], F32, early)
            k_sb = sb("k_sb", [P, 2, C], F32, early)
            v_sb = sb("v_sb", [P, 2, KC, GW], F32, early)
            exp_sb = sb("exp_sb", [P, 2, C], F32, early)
            kvbd = sb("kvbd", [P, KC, OW], F32, early)
            attn = sb("attn", [P, 2, C], F32, early)
            attnT_hi = sb("attnT_hi", [P, KC, P], F32R, early)
            attnT_lo = sb("attnT_lo", [P, KC, P], F32R, early)
            zeros = sb("zeros", [P, TABLE * 2 // P], I32, early)
            den = sb("den", [P, NH], F32, early)
            zden = sb("zden", [P, NH], F32, early)
        with ExitStack() as raws:
            ew = sb("ew", [P, E, 2, KC, C], F32R, raws)
        ew_raw = [sb(f"ew_raw{e}", [P, 2, KC, C]) for e in range(E)]
        rows = sb("rows", [P, 2, C])
        y_sb = sb("y_sb", [P, 2, C])
        bias_bd = sb("bias_bd", [P, 4, C], F32R)
        bias_raw = sb("bias_raw", [P, C])
        bias_hi = sb("bias_hi", [P, C], F32R)
        bias_lo = sb("bias_lo", [P, C])
        gT = sb("gT", [P, NT // 4, P], F32R)
        gates = sb("gates", [P, NT, E])
        gate4 = sb("gate4", [P, NT, 4 * E], F32R)
        y_at = sb("y_at", [P, TOP, NT], I32)
        first_p = sb("first_p", [P, E])
        before = sb("before", [P, E, E])
        is_past = sb("is_past", [1, NS, E - 1])
        past_w = sb("past_w", [1, NS, E - 1])
        plan_f = sb("plan_f", [1, 2, NS])
        plan = sb("plan", [1, 2, NS], I32)
        slot_in = sb("slot_in", [P, NS, 2], I32)

        ident, minus_half = cst[:, COL["IDENT"]], cst[:, COL["HALF"]][:, 0:1]
        ones, tri = cst[:, COL["ONES"]], cst[:, COL["TRI"]]
        rank = cst[:, COL["RANK"]].rearrange("p (t e) -> p t e", e=E)
        ebase = cst[:, COL["EBASE"]].rearrange("p (t e) -> p t e", e=E)

        ps = ctx.enter_context(nc.psum_tensor("ps", [P, 8, C], F32))
        B_WO, B_KV, B_OUT, B_X1 = 2, 3, 5, 7
        kv_ps = ps[:, B_KV:B_KV + 2, 0:2 * GW].rearrange("p b (g n) -> p b g n", g=2)
        kvbd_v = kvbd[:, :, :].rearrange("p (b g) n -> p b g n", g=2)
        PLACE, COUNT = slice(64, 64 + TPB * E), slice(128, 128 + E)

        def out_bank(m):
            return 0 if m >= NT - TPB and m % 2 else B_OUT

        def out_ps(m):
            b = out_bank(m)
            return ps[:, b:b + 2, 0:2 * OW].rearrange("p b (g n) -> p b g n", g=2)

        cst_in, gate_in, x_in, bias_in = sem("cst_in"), sem("gate_in"), sem("x_in"), sem("bias_in")
        w_in = [sem(f"w{n}_in") for n in "kvqo"]
        xT_in = [sem(f"xT{i}_in") for i in range(TPB)]
        ew_in = [sem(f"ew{e}_in") for e in range(E)]
        x1_stored, table_zeroed, scattered = sem("x1_stored"), sem("table_zeroed"), sem("scattered")
        NQ = 8
        slot_in_done = [sem(f"slot_in{q}") for q in range(NQ)]
        rows_in = [sem("rows_in0"), sem("rows_in1")]
        y_stored = [sem("y_stored0"), sem("y_stored1")]
        added = [[sem(f"added{c}_{q}") for q in range(4)] for c in range(TOP)]
        stored = [sem("stored0"), sem("stored1")]
        zeroed = sem("zeroed")
        zeros_ready = sem("zeros_ready")
        xT_hi_ready, xT_ready = sem("xT_hi_ready"), sem("xT_ready")
        w_hi_ready, w_ready = sem("w_hi_ready"), sem("w_ready")
        ew_hi_ready = sem("ew_hi_ready")
        ew_ready = sem("ew_ready")
        gate_hi_ready, gate_ready = sem("gate_hi_ready"), sem("gate_ready")
        proj_done, exp_done, kq_taken, kq_ready = sem("proj_done"), sem("exp_done"), sem("kq_taken"), sem("kq_ready")
        v_ready, kv_done, kvbd_ready = sem("v_ready"), sem("kv_done"), sem("kvbd_ready")
        out_done, den_ready, z_ready, attn_ready = sem("out_done"), sem("den_ready"), sem("z_ready"), sem("attn_ready")
        tr_done, attnT_hi_ready, attnT_ready = sem("tr_done"), sem("attnT_hi_ready"), sem("attnT_ready")
        wo_done, h_ready = sem("wo_done"), sem("h_ready")
        stats_ready, mv_ready, var_ready = sem("stats_ready"), sem("mv_ready"), sem("var_ready")
        rstd_ready, norm_ready, x1_ready = sem("rstd_ready"), sem("norm_ready"), sem("x1_ready")
        x1tr_done, x1T_hi_ready, x1T_ready = sem("x1tr_done"), sem("x1T_hi_ready"), sem("x1T_ready")
        logits_done, logits_read, step, diff_ready = sem("logits_done"), sem("logits_read"), sem("step"), sem("diff_ready")
        expd_ready, chosen_ready, place_done = sem("expd_ready"), sem("chosen_ready"), sem("place_done")
        place_read, entry_ready, plan_ready, y_at_ready = sem("place_read"), sem("entry_ready"), sem("plan_ready"), sem("y_at_ready")
        gate4_ready, gtr_done, gT_ready = sem("gate4_ready"), sem("gtr_done"), sem("gT_ready")
        rowtr_done, rowT_hi_ready, rowT_ready = sem("rowtr_done"), sem("rowT_hi_ready"), sem("rowT_ready")
        y_done, y_used = sem("y_done"), sem("y_used")
        bias_hi_ready, bias_done, bias_used, bstep = sem("bias_hi_ready"), sem("bias_done"), sem("bias_used"), sem("bstep")
        y_out = sem("y_out")

        ew_src = expert_w.rearrange("e (k p) o -> e p k o", p=P)

        def kq_number(kind, i):
            return KQ.index((kind, i)) + 1

        def at_least(eng, semaphore, value):
            if value > 0:
                eng.wait_ge(semaphore, value)

        block = ctx.enter_context(nc.Block())

        @block.sync
        def _(sp):
            def load_xT(b, i):
                at_least(sp, xT_ready, TPB * (b - 1) + i + 1 if b else 0)
                sp.dma_start(x_raw[:, i, :, :], xT[TPB * b + i].rearrange("p (k t) -> p k t", k=KC))\
                    .then_inc(xT_in[i], 16)

            def load_w(m, src, dst):
                for k in range(KC):
                    sp.dma_start(dst[:, k, :], src[:, k, :]).then_inc(w_in[m], 16)

            def load_expert(e):
                sp.dma_start(ew_raw[e][:, LOP], ew_src[e]).then_inc(ew_in[e], 16)

            load_xT(0, 0)
            load_w(0, wkT, w_raw[0][:, LOP])
            load_w(1, wvT, w_raw[1][:, LOP])
            for i in range(1, TPB):
                load_xT(0, i)
            load_w(2, wqT, w_raw[2][:, LOP])
            load_w(3, woT, wo_raw[:, LOP])
            sp.dma_start(acc[:, :, :], x.rearrange("(t p) c -> p t c", p=P)).then_inc(x_in, 16)
            sp.wait_ge(zeros_ready, 1)
            sp.dma_start(table.rearrange("(p r) n -> p (r n)", p=P), zeros[:, :]).then_inc(table_zeroed, 16)
            load_expert(0)
            load_expert(1)
            for name, b, i in TODO:
                if name == "x":
                    load_xT(b, i)
                if name == "nx":
                    m = TPB * b + i
                    sp.wait_ge(x1_ready, m + 1)
                    sp.dma_start(x1_rows[m * P:(m + 1) * P, :], acc[:, m, :]).then_inc(x1_stored, 16)
                if (name, b, i) == ("V", NB - 1, 3):
                    sp.wait_ge(proj_done, NCH * NB)
                    for e in range(2, 6):
                        load_expert(e)
            sp.wait_ge(wo_done, NT)
            load_expert(6)
            load_expert(7)
            for r in range(P // E):
                sp.dma_start(bias_raw[r * E:(r + 1) * E, :], expert_b).then_inc(bias_in, 16)
            sp.wait_ge(plan_ready, 1)
            sp.wait_ge(scattered, 16 * TOP * NT)
            for s in range(NS):
                row = sp.value_load(plan[0:1, 1, s:s + 1], min_val=0, max_val=TABLE - P)
                at_least(sp, slot_in_done[s % NQ], 16 * (s // NQ))
                sp.dma_start(slot_in[:, s, :], table[ds(row, P), :]).then_inc(slot_in_done[s % NQ], 16)
            for s in range(2):
                sp.wait_ge(y_used, s + 1)
                sp.dma_start(y_rows[s * P:(s + 1) * P, :], y_sb[:, s, :]).then_inc(y_stored[s], 16)
            with sp.Fori(1, NS // 2) as j:
                for q in range(2):
                    sp.wait_ge(y_used, 2 * j + q + 1)
                    sp.dma_start(y_rows[ds((2 * j + q) * P, P), :], y_sb[:, q, :]).then_inc(y_stored[q], 16)
            sp.wait_ge(y_used, NS)
            sp.dma_start(y_rows[(NS - 1) * P:NS * P, :], y_sb[:, 0, :]).then_inc(y_stored[0], 16)
            for t in range(NT):
                sp.wait_ge(y_out, t + 1)
                sp.dma_start(out[t * P:(t + 1) * P, :], y_sb[:, t % 2, :]).then_inc(stored[t % 2], 16)
            for s in stored:
                sp.wait_ge(s, 16 * (NT // 2))

        @block.gpsimd
        def _(pool):
            pool.dma_start(cst[:, :], consts).then_inc(cst_in, 16)
            pool.dma_start(gate_raw[:, :, :], gateT).then_inc(gate_in, 16)
            pool.dma_start(ids[:, :], token_ids).then_inc(gate_in, 16)
            nc.gpsimd.memset(kvbd[:, :, :], 0.0).then_inc(zeroed, 1)
            nc.gpsimd.memset(v_sb[:, :, :, :], 1.0).then_inc(zeroed, 1)
            nc.gpsimd.memset(zeros[:, :], 0).then_inc(zeros_ready, 1)

            def power(n):
                pool.wait_ge(var_ready, n + 1)
                nc.gpsimd.tensor_tensor(rstd[:, :], var_eps[:, :], minus_half, ALU.pow).then_inc(rstd_ready, 1)

            def enter(b):
                pool.wait_ge(entry_ready, b + 1)
                for t in range(TPB * b, TPB * b + TPB):
                    for c in range(TOP):
                        pool.indirect_dma_start(
                            out=table, out_offset=bass.IndirectOffsetOnAxis(ap=entry_at[:, c, t:t + 1], axis=0),
                            in_=entry[:, t, c, :], in_offset=None).then_inc(scattered, 16)

            pool.wait_ge(cst_in, 16)
            pool.wait_ge(table_zeroed, 16)
            for name, b, i in TODO:
                if name == "wo":
                    power(TPB * b + i)
                if name == "rt":
                    enter(b)
                if name == "we":
                    pool.wait_ge(ew_hi_ready, b + 1)
                    nc.gpsimd.tensor_tensor(ew[:, b, LOP], ew_raw[b][:, LOP], ew[:, b, HIP].bitcast(F32),
                                            ALU.subtract).then_inc(ew_ready, 1)
            pool.wait_ge(x1_stored, 16 * NT)
            for s in range(NS):
                pool.wait_ge(slot_in_done[s % NQ], 16 * (s // NQ + 1))
                at_least(pool, rowtr_done, s - 1)
                pool.indirect_dma_start(
                    out=rows[:, s % 2, :], out_offset=None, in_=x1_rows,
                    in_offset=bass.IndirectOffsetOnAxis(ap=slot_in[:, s, 0:1], axis=0)).then_inc(rows_in[s % 2], 16)
            pool.wait_ge(y_at_ready, 1)
            for s in range(2):
                pool.wait_ge(y_stored[s], 16 * ((NS + 1 - s) // 2))

            def add(c, t):
                if c == 0:
                    pool.wait_ge(bias_used, t + 1)
                else:
                    pool.wait_ge(added[0][t % 4], 16 * (t // 4 + 1))
                pool.indirect_dma_start(
                    out=acc[:, t, :], out_offset=None, in_=y_rows,
                    in_offset=bass.IndirectOffsetOnAxis(ap=y_at[:, c, t:t + 1], axis=0),
                    compute_op=ALU.add).then_inc(added[c][t % 4], 16)

            for t in range(NT + 2):
                if t < NT:
                    add(0, t)
                if t >= 2:
                    add(1, t - 2)
                if t >= 5:
                    power(NT + t - 5)
            for t in range(NT - 3, NT):
                power(NT + t)

        @block.scalar
        def _(act):
            def split_x(b, i):
                tok = slice(i * P, (i + 1) * P)
                act.wait_ge(xT_in[i], 16 * b + 16)
                at_least(act, proj_done, NCH * b - (2 if i < 3 else 0) if b else 0)
                nc.scalar.copy(xT_hi[:, :, tok], x_raw[:, i, :, :]).then_inc(xT_hi_ready, 1)

            def split_w(m, hl, raw):
                for k in range(KC):
                    if k == 0:
                        act.wait_ge(w_in[m], 16 * KC)
                    nc.scalar.copy(hl[:, HIP, k, :], raw[:, LOP, k, :]).then_inc(w_hi_ready, 1)

            def split_expert(e):
                act.wait_ge(ew_in[e], 16)
                nc.scalar.copy(ew[:, e, HIP], ew_raw[e][:, LOP]).then_inc(ew_hi_ready, 1)

            def exp_of(b, kind, i):
                at, n = CHUNKS.index((kind, i)), kq_number(kind, i)
                act.wait_ge(proj_done, NCH * b + at + 1)
                at_least(act, kq_ready, NKQ * b + n - 2)
                nc.scalar.activation(exp_sb[:, n % 2, :], ps[:, at % 2, :], ACT.Exp).then_inc(exp_done, 1)

            def take_v(b, i):
                at = CHUNKS.index(("V", i))
                act.wait_ge(proj_done, NCH * b + at + 1)
                act.wait_ge(zeroed, 2)
                at_least(act, kv_done, TPB * b + i - 1)
                nc.scalar.copy(v_sb[:, i % 2, :, 0:P],
                               ps[:, at % 2, :].rearrange("p (g n) -> p g n", g=KC)).then_inc(v_ready, 1)

            def attnT_high(m):
                act.wait_ge(tr_done, m + 1)
                at_least(act, wo_done, m)
                nc.scalar.copy(attnT_hi[:, :, :], ps[:, out_bank(m), :].rearrange("p (k t) -> p k t", k=KC))\
                    .then_inc(attnT_hi_ready, 1)

            split_x(0, 0)
            split_w(0, w_hl[:, 0], w_raw[0])
            split_w(1, w_hl[:, 1], w_raw[1])
            for i in range(1, TPB):
                split_x(0, i)
            split_w(2, w_hl[:, 2], w_raw[2])
            act.wait_ge(gate_in, 32)
            nc.scalar.copy(gate_hl[:, :, 0:E], gate_raw[:, :, :]).then_inc(gate_hi_ready, 1)
            for name, b, i in TODO:
                m = TPB * b + i
                if name in ("K", "Q"):
                    exp_of(b, name, i)
                elif name == "V":
                    take_v(b, i)
                elif name == "wo_w":
                    split_w(3, wo_hl, wo_raw)
                elif name == "x":
                    split_x(b, i)
                elif name == "we":
                    split_expert(b)
                elif name == "tr":
                    attnT_high(m)
                elif name == "nx":
                    act.wait_ge(norm_ready, m + 1)
                    nc.scalar.activation(acc[:, m, :], acc[:, m, :], ACT.Identity, bias=nbias[:, :],
                                         scale=rstd[:, :]).then_inc(x1_ready, 1)
                elif name == "xt":
                    act.wait_ge(x1tr_done, m + 1)
                    at_least(act, logits_done, m - 1)
                    nc.scalar.copy(rowT_hi[:, m % 2, :, :], ps[:, B_X1, :].rearrange("p (k t) -> p k t", k=KC))\
                        .then_inc(x1T_hi_ready, 1)
                elif name == "gt":
                    act.wait_ge(diff_ready, b + 1)
                    nc.scalar.activation(g2[:, :], diff[:, :], ACT.Exp).then_inc(expd_ready, 1)
            for e in range(4, E):
                split_expert(e)
            act.wait_ge(bias_in, 16 * (P // E))
            nc.scalar.copy(bias_hi[:, :], bias_raw[:, :]).then_inc(bias_hi_ready, 1)
            act.wait_ge(gtr_done, 1)
            nc.scalar.copy(gT[:, :, :], ps[:, 5, :].rearrange("p (q t) -> p q t", q=NT // 4)).then_inc(gT_ready, 1)

            def row_high(s, q):
                act.wait_ge(rowtr_done, s + 1)
                if not isinstance(s, int) or s >= 2:
                    act.wait_ge(y_done, s - 1)
                nc.scalar.copy(rowT_hi[:, q, :, :], ps[:, 6 + q, :].rearrange("p (k t) -> p k t", k=KC))\
                    .then_inc(rowT_hi_ready, 1)

            for s in range(4):
                row_high(s, s % 2)
            with act.Fori(2, NS // 2) as j:
                row_high(2 * j, 0)
                row_high(2 * j + 1, 1)
            row_high(NS - 1, 0)
            for t in range(NT):
                act.wait_ge(norm_ready, NT + t + 1)
                if t < 2:
                    act.wait_ge(y_stored[t], 16 * ((NS + 1 - t) // 2))
                at_least(act, stored[t % 2], 16 * (t // 2))
                nc.scalar.activation(y_sb[:, t % 2, :], acc[:, t, :], ACT.Identity, bias=nbias[:, :],
                                     scale=rstd[:, :]).then_inc(y_out, 1)

        @block.vector
        def _(dve):
            steps = [0]

            def link(ins):
                steps[0] += 1
                ins.then_inc(step, 1)
                dve.wait_ge(step, steps[0])

            def split_x(b, i):
                tok = slice(i * P, (i + 1) * P)
                dve.wait_ge(xT_hi_ready, TPB * b + i + 1)
                nc.vector.tensor_tensor(xT_lo[:, :, tok], x_raw[:, i, :, :], xT_hi[:, :, tok].bitcast(F32),
                                        ALU.subtract).then_inc(xT_ready, 1)

            def split_w(m, hl, raw):
                for k in range(KC):
                    dve.wait_ge(w_hi_ready, m * KC + k + 1)
                    nc.vector.tensor_tensor(hl[:, LOP, k, :], raw[:, LOP, k, :], hl[:, HIP, k, :].bitcast(F32),
                                            ALU.subtract).then_inc(w_ready, 1)

            def feature_map(b, kind, i):
                at, n = CHUNKS.index((kind, i)), kq_number(kind, i)
                if kind == "K":
                    dst = k_sb[:, i % 2, :]
                    at_least(dve, kv_done, TPB * b + i - 1)
                else:
                    dst = q_sb[:, b % 2, i, :]
                    at_least(dve, out_done, TPB * (b - 1))
                dve.wait_ge(exp_done, NKQ * b + n)
                nc.vector.tensor_scalar(dst, ps[:, at % 2, :], 0.0, None, ALU.max).then_inc(kq_taken, 1)
                dve.wait_ge(kq_taken, NKQ * b + n)
                nc.vector.scalar_tensor_tensor(out=dst, in0=exp_sb[:, n % 2, :], scalar=1.0, in1=dst,
                                               op0=ALU.min, op1=ALU.add).then_inc(kq_ready, 1)

            def take_kv(b):
                dve.wait_ge(kv_done, TPB * b + TPB)
                dve.wait_ge(zeroed, 2)
                at_least(dve, out_done, TPB * b)
                for j in range(HG):
                    h = slice(j * DH, (j + 1) * DH)
                    nc.vector.tensor_copy(kvbd_v[h, :, :, h], kv_ps[h, :, :, h]).then_inc(kvbd_ready, 1)
                    nc.vector.tensor_copy(kvbd_v[h, :, :, P + j:P + j + 1], kv_ps[h, :, :, P:P + 1])\
                        .then_inc(kvbd_ready, 1)

            def take_out(m):
                src = out_ps(m)
                dve.wait_ge(out_done, m + 1)
                nc.vector.tensor_scalar(den[:, :].rearrange("p (b g h) -> p b g h", b=2, g=2),
                                        src[:, :, :, P:OW], 1e-6, None, ALU.add).then_inc(den_ready, 1)
                dve.wait_ge(den_ready, m + 1)
                nc.vector.reciprocal(zden[:, :], den[:, :]).then_inc(z_ready, 1)
                dve.wait_ge(z_ready, m + 1)
                at_least(dve, tr_done, m - 1)
                for c in range(2):
                    half = slice(c * 2 * P, (c + 1) * 2 * P)
                    nc.vector.tensor_tensor(
                        attn[:, m % 2, half].rearrange("p (g h e) -> p g h e", g=2, h=HG),
                        src[:, c, :, 0:P].rearrange("p g (h e) -> p g h e", h=HG),
                        zden[:, c * 8:c * 8 + 8].rearrange("p (g h) -> p g h", g=2).unsqueeze(3)
                        .to_broadcast([P, 2, HG, DH]), ALU.mult).then_inc(attn_ready, 1)

            def attnT_low(m):
                dve.wait_ge(attnT_hi_ready, m + 1)
                nc.vector.tensor_tensor(attnT_lo[:, :, :], ps[:, out_bank(m), :].rearrange("p (k t) -> p k t", k=KC),
                                        attnT_hi[:, :, :].bitcast(F32), ALU.subtract).then_inc(attnT_ready, 1)

            def statistics(n, a):
                nc.vector.bn_stats(stats[:, :], a).then_inc(stats_ready, 1)
                dve.wait_ge(stats_ready, n + 1)
                nc.vector.bn_aggr(mv[:, :], stats[:, :]).then_inc(mv_ready, 1)
                dve.wait_ge(mv_ready, n + 1)
                nc.vector.tensor_scalar(var_eps[:, :], mv[:, 1:2], EPS, None, ALU.add).then_inc(var_ready, 1)

            def norm_bias(n):
                dve.wait_ge(rstd_ready, n + 1)
                nc.vector.tensor_scalar(nbias[:, :], mv[:, 0:1], rstd[:, 0:1], -1.0, ALU.mult, ALU.mult)\
                    .then_inc(norm_ready, 1)

            def take_wo(m):
                dve.wait_ge(wo_done, m + 1)
                a = acc[:, m, :]
                nc.vector.tensor_tensor(a, ps[:, B_WO, :], a, ALU.add).then_inc(h_ready, 1)
                dve.wait_ge(h_ready, m + 1)
                at_least(dve, x1_ready, m)
                statistics(m, a)

            def argmax(one, top):
                w, p = work[:, 0:TPB, :], pick[:, 0:TPB]
                link(nc.vector.tensor_reduce(top[:, :], w, AX_X, ALU.max))
                link(nc.vector.tensor_tensor(one, w, top[:, :].unsqueeze(2).to_broadcast([P, TPB, E]), ALU.is_equal))
                link(nc.vector.tensor_tensor(one, one, rank, ALU.mult))
                link(nc.vector.tensor_reduce(p, one, AX_X, ALU.max))
                link(nc.vector.tensor_tensor(one, one, p.unsqueeze(2).to_broadcast([P, TPB, E]), ALU.is_equal))

            def choose(b):
                at = slice(TPB * b, TPB * b + TPB)
                w, o1, o2 = work[:, 0:TPB, :], one1[:, at, :], one2[:, at, :]
                dve.wait_ge(logits_read, TPB * b + TPB)
                link(nc.vector.tensor_copy(w, logit[:, :, :]))
                argmax(o1, top1)
                link(nc.vector.tensor_scalar(w, o1, -3.0e38, None, ALU.mult))
                link(nc.vector.tensor_tensor(w, w, logit[:, :, :], ALU.add))
                argmax(o2, top2)
                nc.vector.tensor_tensor(diff[:, :], top2[:, :], top1[:, :], ALU.subtract).then_inc(diff_ready, 1)
                nc.vector.tensor_tensor(chosen[:, at, :], o1, o2, ALU.add).then_inc(chosen_ready, 1)
                dve.wait_ge(chosen_ready, (TPB + 1) * b + 1)
                for t in range(TPB * b, TPB * b + TPB):
                    nc.vector.tensor_tensor(earlier[:, t + 1, :], earlier[:, t, :], chosen[:, t, :], ALU.add)\
                        .then_inc(chosen_ready, 1)
                    dve.wait_ge(chosen_ready, (TPB + 1) * b + 2 + t - TPB * b)
                dve.wait_ge(expd_ready, b + 1)
                link(nc.vector.tensor_scalar(g1[:, :], g2[:, :], 1.0, None, ALU.add))
                link(nc.vector.reciprocal(g1[:, :], g1[:, :]))
                link(nc.vector.tensor_tensor(g2[:, :], g2[:, :], g1[:, :], ALU.mult))
                for c, g in enumerate((g1, g2)):
                    link(nc.vector.tensor_copy(entry[:, at, c, 1].bitcast(F32), g[:, :]))
                    link(nc.vector.tensor_copy(entry[:, at, c, 0], ids[:, at]))

            def enter(b):
                at = slice(TPB * b, TPB * b + TPB)
                w = work[:, 0:TPB, :]
                dve.wait_ge(place_done, b + 1)
                nc.vector.tensor_copy(place[:, at, :], ps[:, B_X1, PLACE].rearrange("p (t e) -> p t e", e=E))\
                    .then_inc(place_read, 1)
                dve.wait_ge(place_read, b + 1)
                for c, one in enumerate((one1, one2)):
                    link(nc.vector.tensor_tensor(w, place[:, at, :], ebase, ALU.add))
                    link(nc.vector.tensor_tensor(w, w, one[:, at, :], ALU.mult))
                    link(nc.vector.tensor_reduce(pick[:, 0:TPB], w, AX_X, ALU.add))
                    last = nc.vector.tensor_copy(entry_at[:, c, at], pick[:, 0:TPB])
                    if c == 0:
                        link(last)
                last.then_inc(entry_ready, 1)

            dve.wait_ge(cst_in, 16)
            link(nc.vector.memset(earlier[:, 0, :], 0.0))
            split_x(0, 0)
            split_w(0, w_hl[:, 0], w_raw[0])
            split_w(1, w_hl[:, 1], w_raw[1])
            for i in range(1, TPB):
                split_x(0, i)
            split_w(2, w_hl[:, 2], w_raw[2])
            dve.wait_ge(gate_hi_ready, 1)
            nc.vector.tensor_tensor(gate_hl[:, :, E:2 * E], gate_raw[:, :, :], gate_hl[:, :, 0:E].bitcast(F32),
                                    ALU.subtract).then_inc(gate_ready, 1)
            for name, b, i in TODO:
                m = TPB * b + i
                if name in ("K", "Q"):
                    feature_map(b, name, i)
                elif name == "wo_w":
                    split_w(3, wo_hl, wo_raw)
                elif name == "x":
                    split_x(b, i)
                elif name == "kv" and i == TPB - 1:
                    take_kv(b)
                elif name == "out":
                    take_out(m)
                elif name == "tr":
                    attnT_low(m)
                elif name == "wo":
                    if m == 0:
                        dve.wait_ge(x_in, 16)
                    take_wo(m)
                elif name == "nx":
                    norm_bias(m)
                elif name == "xt":
                    dve.wait_ge(x1T_hi_ready, m + 1)
                    nc.vector.tensor_tensor(rowT_lo[:, m % 2, :, :], ps[:, B_X1, :].rearrange("p (k t) -> p k t", k=KC),
                                            rowT_hi[:, m % 2, :, :].bitcast(F32), ALU.subtract).then_inc(x1T_ready, 1)
                elif name == "lg":
                    dve.wait_ge(logits_done, m + 1)
                    nc.vector.tensor_reduce(logit[:, i, :], ps[:, B_X1, 0:2 * E].rearrange("p (a e) -> p e a", a=2),
                                            AX_X, ALU.add).then_inc(logits_read, 1)
                elif name == "gt":
                    choose(b)
                elif name == "rt":
                    enter(b)

            link(nc.vector.tensor_scalar(tiles_i[:, :], ps[:, B_X1, COUNT], float(P - 1), None, ALU.add))
            link(nc.vector.tensor_scalar(tiles_i[:, :], tiles_i[:, :], P.bit_length() - 1, None,
                                         ALU.logical_shift_right))
            link(nc.vector.tensor_copy(tiles[:, :], tiles_i[:, :]))
            link(nc.vector.tensor_tensor(before[:, :, :], tiles[:, :].unsqueeze(1).to_broadcast([P, E, E]),
                                         cst[:, COL["BEFORE"]].rearrange("p (e f) -> p e f", f=E), ALU.mult))
            link(nc.vector.tensor_reduce(first[:, :], before[:, :, :], AX_X, ALU.add))
            link(nc.vector.tensor_tensor(
                is_past[:, :, :], cst[0:1, COL["SLOT"]].unsqueeze(2).to_broadcast([1, NS, E - 1]),
                first[0:1, 1:E].unsqueeze(1).to_broadcast([1, NS, E - 1]), ALU.is_ge))
            link(nc.vector.tensor_scalar(skip[:, :], tiles[:, :], -float(P), float(REGION), ALU.mult, ALU.add))
            link(nc.vector.tensor_tensor(past_w[:, :, :], is_past[:, :, :],
                                         skip[0:1, 0:E - 1].unsqueeze(1).to_broadcast([1, NS, E - 1]), ALU.mult))
            link(nc.vector.tensor_reduce(plan_f[:, 0, :], is_past[:, :, :], AX_X, ALU.add))
            link(nc.vector.tensor_reduce(plan_f[:, 1, :], past_w[:, :, :], AX_X, ALU.add))
            link(nc.vector.tensor_tensor(plan_f[:, 1, :], plan_f[:, 1, :], cst[0:1, COL["SLOTROW"]], ALU.add))
            nc.vector.tensor_copy(plan[:, :, :], plan_f[:, :, :]).then_inc(plan_ready, 1)
            gate_of = entry[:, :, :, 1].bitcast(F32)
            for c, one in enumerate((one1, one2)):
                to = work if c == 0 else gates
                link(nc.vector.tensor_tensor(to[:, :, :], one[:, :, :],
                                             gate_of[:, :, c].unsqueeze(2).to_broadcast([P, NT, E]), ALU.mult))
            link(nc.vector.tensor_tensor(gates[:, :, :], gates[:, :, :], work[:, :, :], ALU.add))
            link(nc.vector.tensor_copy(gate4[:, :, 0:E], gates[:, :, :]))
            nc.vector.tensor_copy(gate4[:, :, E:2 * E], gates[:, :, :]).then_inc(gate4_ready, 1)
            for q in (2, 3):
                nc.vector.tensor_tensor(gate4[:, :, q * E:(q + 1) * E], gates[:, :, :],
                                        gate4[:, :, 0:E].bitcast(F32), ALU.subtract).then_inc(gate4_ready, 1)
            for e in range(4, E):
                dve.wait_ge(ew_hi_ready, e + 1)
                dve.wait_ge(ew_ready, e)
                nc.vector.tensor_tensor(ew[:, e, LOP], ew_raw[e][:, LOP], ew[:, e, HIP].bitcast(F32),
                                        ALU.subtract).then_inc(ew_ready, 1)

            def row_low(s, q):
                dve.wait_ge(rowT_hi_ready, s + 1)
                nc.vector.tensor_tensor(rowT_lo[:, q, :, :], ps[:, 6 + q, :].rearrange("p (k t) -> p k t", k=KC),
                                        rowT_hi[:, q, :, :].bitcast(F32), ALU.subtract).then_inc(rowT_ready, 1)

            def take_y(s, q):
                dve.wait_ge(y_done, s + 1)
                if not isinstance(s, int):
                    dve.wait_ge(y_stored[q], 16 * ((s - q) // 2) if isinstance(s, int) else s * 8 - 8 * q)
                elif s >= 2:
                    dve.wait_ge(y_stored[q], 16 * (s // 2))
                gate = slot_in[:, s, 1:2] if isinstance(s, int) else slot_in[:, ds(s, 1), 1]
                nc.vector.tensor_scalar(y_sb[:, q, :], ps[:, q, :], gate.bitcast(F32), None, ALU.mult)\
                    .then_inc(y_used, 1)

            row_low(0, 0)
            dve.wait_ge(bias_hi_ready, 1)
            link(nc.vector.tensor_tensor(bias_lo[:, :], bias_raw[:, :], bias_hi[:, :].bitcast(F32), ALU.subtract))
            for j in range(4):
                link(nc.vector.tensor_scalar(bias_bd[:, j, :], bias_lo[:, :], cst[:, COL["LO"]][:, j:j + 1], None,
                                             ALU.mult))
                nc.vector.scalar_tensor_tensor(out=bias_bd[:, j, :], in0=bias_hi[:, :].bitcast(F32),
                                               scalar=cst[:, COL["HI"]][:, j:j + 1],
                                               in1=bias_bd[:, j, :].bitcast(F32), op0=ALU.mult, op1=ALU.add)\
                    .then_inc(bstep, 1)
            row_low(1, 1)
            take_y(0, 0)
            row_low(2, 0)
            take_y(1, 1)
            row_low(3, 1)
            take_y(2, 0)
            link(nc.vector.tensor_scalar(first_p[:, :], first[:, :], float(P), None, ALU.mult))
            for c, one in enumerate((one1, one2)):
                link(nc.vector.tensor_tensor(work[:, :, :], place[:, :, :],
                                             first_p[:, :].unsqueeze(1).to_broadcast([P, NT, E]), ALU.add))
                link(nc.vector.tensor_tensor(work[:, :, :], work[:, :, :], one[:, :, :], ALU.mult))
                link(nc.vector.tensor_reduce(pick[:, :], work[:, :, :], AX_X, ALU.add))
                last = nc.vector.tensor_copy(y_at[:, c, :], pick[:, :])
                if c == 0:
                    link(last)
            last.then_inc(y_at_ready, 1)
            with dve.Fori(2, NS // 2) as j:
                row_low(2 * j, 0)
                take_y(2 * j - 1, 1)
                row_low(2 * j + 1, 1)
                take_y(2 * j, 0)
            row_low(NS - 1, 0)
            take_y(NS - 2, 1)
            take_y(NS - 1, 0)

            def add_bias(t):
                dve.wait_ge(bias_done, t + 1)
                nc.vector.tensor_tensor(acc[:, t, :], ps[:, t % 8, :], acc[:, t, :], ALU.add).then_inc(bias_used, 1)

            dve.wait_ge(x1_stored, 16 * NT)
            for t in range(6):
                add_bias(t)
            for t in range(NT):
                if t + 6 < NT:
                    add_bias(t + 6)
                dve.wait_ge(added[1][t % 4], 16 * (t // 4 + 1))
                dve.wait_ge(y_out, t) if t else dve.wait_ge(x1_ready, NT)
                statistics(NT + t, acc[:, t, :])
                norm_bias(NT + t)

        @block.tensor
        def _(pe):
            def three(bank, lhs_hi, lhs_lo, rhs_hi, rhs_lo, arrived=None):
                for k in range(KC):
                    if arrived is not None:
                        pe.wait_ge(w_ready, arrived + k + 1)
                    nc.tensor.matmul(bank, lhs_hi(k), rhs_hi(k), start=(k == 0), stop=False)
                    nc.tensor.matmul(bank, lhs_hi(k), rhs_lo(k), start=False, stop=False)
                    last = nc.tensor.matmul(bank, lhs_lo(k), rhs_hi(k), start=False, stop=(k == KC - 1))
                return last

            def project(b, kind, i):
                at, w = CHUNKS.index((kind, i)), "KVQ".index(kind)
                pe.wait_ge(xT_ready, TPB * b + (TPB if kind == "Q" else i + 1))
                if b or at >= 2:
                    back, bb = CHUNKS[(at - 2) % NCH], b - (at < 2)
                    if back[0] == "V":
                        pe.wait_ge(v_ready, TPB * bb + back[1] + 1)
                    else:
                        pe.wait_ge(kq_taken, NKQ * bb + kq_number(*back))
                bank, arrived = ps[:, at % 2, :], w * KC if b == 0 and i == 0 else None
                here = slice(i * P, (i + 1) * P)
                if kind == "Q":
                    last = three(bank, lambda k: w_hl[:, w, HIP, k, here], lambda k: w_hl[:, w, LOP, k, here],
                                 lambda k: xT_hi[:, k, :], lambda k: xT_lo[:, k, :], arrived)
                else:
                    last = three(bank, lambda k: xT_hi[:, k, here], lambda k: xT_lo[:, k, here],
                                 lambda k: w_hl[:, w, HIP, k, :], lambda k: w_hl[:, w, LOP, k, :], arrived)
                last.then_inc(proj_done, 1)

            def kv(b, i):
                pe.wait_ge(kq_ready, NKQ * b + kq_number("K", i))
                pe.wait_ge(v_ready, TPB * b + i + 1)
                if i == 0:
                    at_least(pe, kvbd_ready, 2 * HG * b)
                for g in range(KC):
                    last = nc.tensor.matmul(kv_ps[:, g // 2, g % 2, :], k_sb[:, i % 2, g * P:(g + 1) * P],
                                            v_sb[:, i % 2, g, :], start=(i == 0 and g % 2 == 0), stop=(i == TPB - 1),
                                            skip_group_check=True)
                last.then_inc(kv_done, 1)

            def attend(b, m, i):
                dst = out_ps(m)
                pe.wait_ge(kq_ready, NKQ * (b + 1) - 1)
                pe.wait_ge(kvbd_ready, 2 * HG * b + 2 * HG)
                if out_bank(m) == out_bank(m - 1):
                    at_least(pe, attnT_ready, m)
                    at_least(pe, attn_ready, 2 * m)
                elif m == NT - TPB + 1:
                    pe.wait_ge(v_ready, NT)
                    pe.wait_ge(kq_taken, NKQ * NB)
                else:
                    pe.wait_ge(attnT_ready, m - 1)
                    pe.wait_ge(attn_ready, 2 * m - 2)
                for g in range(KC):
                    last = nc.tensor.matmul(dst[:, g // 2, g % 2, :], q_sb[:, b % 2, g, i * P:(i + 1) * P],
                                            kvbd[:, g, :], start=True, stop=True)
                last.then_inc(out_done, 1)

            def turn(m):
                pe.wait_ge(attn_ready, 2 * m + 2)
                for k in range(KC):
                    last = nc.tensor.transpose(ps[:, out_bank(m), k * P:(k + 1) * P],
                                               attn[:, m % 2, k * P:(k + 1) * P], ident)
                last.then_inc(tr_done, 1)

            def output(m):
                pe.wait_ge(attnT_ready, m + 1)
                at_least(pe, h_ready, m)
                three(ps[:, B_WO, :], lambda k: attnT_hi[:, k, :], lambda k: attnT_lo[:, k, :],
                      lambda k: wo_hl[:, HIP, k, :], lambda k: wo_hl[:, LOP, k, :],
                      3 * KC if m == 0 else None).then_inc(wo_done, 1)

            def turn_x1(m):
                pe.wait_ge(x1_ready, m + 1)
                at_least(pe, logits_read, m)
                at_least(pe, place_read, m // TPB)
                for k in range(KC):
                    last = nc.tensor.transpose(ps[:, B_X1, k * P:(k + 1) * P], acc[:, m, k * P:(k + 1) * P], ident)
                last.then_inc(x1tr_done, 1)

            def logits(m):
                pe.wait_ge(x1T_ready, m + 1)
                to = ps[:, B_X1, 0:2 * E]
                for k in range(KC):
                    nc.tensor.matmul(to, rowT_hi[:, m % 2, k, :], gate_hl[:, k, :], start=(k == 0), stop=False)
                    last = nc.tensor.matmul(to, rowT_lo[:, m % 2, k, :], gate_hl[:, k, :], start=False,
                                            stop=(k == KC - 1))
                last.then_inc(logits_done, 1)

            def places(b):
                at = slice(TPB * b, TPB * b + TPB)
                pe.wait_ge(chosen_ready, (TPB + 1) * (b + 1))
                to = ps[:, B_X1, PLACE]
                if b == NB - 1:
                    nc.tensor.matmul(ps[:, B_X1, COUNT], ones, earlier[:, NT, :], start=True, stop=True)
                nc.tensor.matmul(to, tri, chosen[:, at, :].rearrange("p t e -> p (t e)"), start=True, stop=False)
                nc.tensor.matmul(to, ones, earlier[:, at, :].rearrange("p t e -> p (t e)"), start=False, stop=True)\
                    .then_inc(place_done, 1)

            pe.wait_ge(cst_in, 16)
            for name, b, i in TODO:
                m = TPB * b + i
                if name in ("K", "V", "Q"):
                    project(b, name, i)
                elif name == "kv":
                    kv(b, i)
                elif name == "out":
                    attend(b, m, i)
                elif name == "tr":
                    turn(m)
                elif name == "wo":
                    output(m)
                elif name == "xt":
                    turn_x1(m)
                elif name == "lg":
                    if m == 0:
                        pe.wait_ge(gate_ready, 1)
                    logits(m)
                elif name == "rt":
                    places(b)

            pe.wait_ge(gate4_ready, 3)
            for q in range(NT // 4):
                last = nc.tensor.transpose(ps[:, 5, q * P:(q + 1) * P],
                                           gate4[:, 4 * q:4 * q + 4, :].rearrange("p t r -> p (t r)").bitcast(F32),
                                           ident)
            last.then_inc(gtr_done, 1)

            def turn_rows(s, q, nth):
                pe.wait_ge(rows_in[q], nth)
                if not isinstance(s, int) or s >= 2:
                    pe.wait_ge(rowT_ready, s - 1)
                for k in range(KC):
                    last = nc.tensor.transpose(ps[:, 6 + q, k * P:(k + 1) * P], rows[:, q, k * P:(k + 1) * P], ident)
                last.then_inc(rowtr_done, 1)

            def expert(s, q):
                e = pe.value_load(plan[0:1, 0, s:s + 1] if isinstance(s, int) else plan[0:1, 0, ds(s, 1)],
                                  min_val=0, max_val=E - 1)
                pe.wait_ge(ew_ready, e + 1)
                pe.wait_ge(rowT_ready, s + 1)
                if not isinstance(s, int) or s >= 2:
                    pe.wait_ge(y_used, s - 1)
                three(ps[:, q, :], lambda k: rowT_hi[:, q, k, :], lambda k: rowT_lo[:, q, k, :],
                      lambda k: ew[:, ds(e, 1), HIP, k, :], lambda k: ew[:, ds(e, 1), LOP, k, :]).then_inc(y_done, 1)

            pe.wait_ge(plan_ready, 1)
            turn_rows(0, 0, 16)
            turn_rows(1, 1, 16)
            expert(0, 0)
            turn_rows(2, 0, 32)
            expert(1, 1)
            turn_rows(3, 1, 32)
            expert(2, 0)
            with pe.Fori(2, NS // 2) as j:
                turn_rows(2 * j, 0, 16 * j + 16)
                expert(2 * j - 1, 1)
                turn_rows(2 * j + 1, 1, 16 * j + 16)
                expert(2 * j, 0)
            turn_rows(NS - 1, 0, 16 * (NS // 2) + 16)
            expert(NS - 2, 1)
            expert(NS - 1, 0)
            pe.wait_ge(bstep, 4)
            pe.wait_ge(gT_ready, 1)
            pe.wait_ge(y_used, NS)
            for t in range(NT):
                at_least(pe, bias_used, t - 7)
                nc.tensor.matmul(ps[:, t % 8, :], gT[:, t // 4, :], bias_bd[:, t % 4, :],
                                 start=True, stop=True).then_inc(bias_done, 1)


_INS = ["x", "xT", "wkT", "wvT", "wqT", "woT", "gateT", "expert_w", "expert_b", "consts", "token_ids"]


def kernel(L0_attn_x, L0_attn_cos, L0_attn_sin, L0_attn_Wq, L0_attn_Wk, L0_attn_Wv, L0_attn_Wo,
           L0_ffn_gate_w, L0_ffn_expert_w, L0_ffn_expert_b):
    import numpy as np
    import concourse.bacc as bacc
    from concourse.bass_utils import run_bass_kernel_spmd

    x = np.asarray(L0_attn_x)
    B, T, C = x.shape
    rows = np.ascontiguousarray(x.reshape(B * T, C))

    def by_block(w):
        w = np.asarray(w)
        return np.ascontiguousarray(w.reshape(w.shape[0], C // P, P).transpose(2, 1, 0))

    E = N_EXPERTS
    part, f32 = np.arange(P), np.float32
    consts = np.zeros((P, C_END), f32)
    consts[:, COL["IDENT"]] = np.eye(P, dtype=f32)
    consts[:, COL["TRI"]] = part[:, None] < part[None, :]
    consts[:, COL["ONES"]] = 1
    consts[:, COL["RANK"]] = np.tile(np.arange(E, 0, -1), 4)
    consts[:, COL["EBASE"]] = np.tile(np.arange(E) * REGION, 4)
    consts[:, COL["BEFORE"]] = (np.arange(E)[None, :] < np.arange(E)[:, None]).reshape(-1)
    consts[:, COL["SLOT"]] = np.arange(NS)
    consts[:, COL["SLOTROW"]] = np.arange(NS) * P
    consts[:, COL["HI"]] = (part[:, None] // 32 == np.arange(4)) & (part[:, None] // E % 2 == 0)
    consts[:, COL["LO"]] = (part[:, None] // 32 == np.arange(4)) & (part[:, None] // E % 2 == 1)
    consts[:, COL["HALF"]] = -0.5
    arrays = {
        "x": rows,
        "xT": np.ascontiguousarray(rows.reshape(-1, P, C // P, P).transpose(0, 3, 2, 1)).reshape(-1, P, C),
        "wkT": by_block(L0_attn_Wk), "wvT": by_block(L0_attn_Wv),
        "wqT": by_block(L0_attn_Wq), "woT": by_block(L0_attn_Wo),
        "gateT": by_block(L0_ffn_gate_w),
        "expert_w": np.asarray(L0_ffn_expert_w), "expert_b": np.asarray(L0_ffn_expert_b),
        "consts": consts,
        "token_ids": np.ascontiguousarray(np.arange(B * T, dtype=np.int32).reshape(-1, P).T),
    }
    nc = bacc.Bacc("TRN2", target_bir_lowering=False, num_devices=1)
    args = [nc.dram_tensor(n, arrays[n].shape, I32 if n == "token_ids" else F32, kind="ExternalInput").ap()
            for n in _INS]
    out = nc.dram_tensor("out", rows.shape, F32, kind="ExternalOutput").ap()
    build(nc, *args, out)
    r = run_bass_kernel_spmd(nc, [arrays], core_ids=[0])
    return r.results[0]["out"].reshape(B, T, C)
```

```python
from contextlib import ExitStack

import concourse.bass as bass
from concourse import mybir

F32 = mybir.dt.float32
F32R = mybir.dt.float32r
I32 = mybir.dt.int32
ALU = mybir.AluOpType
ACT = mybir.ActivationFunctionType
AX_X = mybir.AxisListType.X
ds = bass.ds

P = 128
N_EXPERTS, N_TOKENS, TOP = 8, 2048, 2
NS = TOP * N_TOKENS // P + N_EXPERTS - 1
REGION = N_TOKENS
TABLE = N_EXPERTS * REGION + N_EXPERTS * P
ENTRY = 3

_widths = [("IDENT", P), ("TRI", P), ("ONES", P), ("RANK", 4 * N_EXPERTS), ("EBASE", 4 * N_EXPERTS),
           ("BEFORE", N_EXPERTS ** 2), ("SLOT", NS), ("SLOTROW", NS), ("HI", 1), ("LO", 1), ("HALF", 2)]
COL, C_END = {}, 0
for _n, _w in _widths:
    COL[_n] = slice(C_END, C_END + _w)
    C_END += _w

NB, TPB = 4, 4
NT = NB * TPB

_first = [("K", 0), ("V", 0), ("K", 1), ("V", 1), ("Q", 0), ("K", 2), ("V", 2), ("Q", 1), ("Q", 2),
          ("Q", 3), ("K", 3), ("V", 3)]
_mixed = [("K", 0), ("V", 0), ("Q", 0), ("K", 1), ("V", 1), ("Q", 1), ("K", 2), ("V", 2), ("Q", 2),
          ("Q", 3), ("K", 3), ("V", 3)]
_last = [("K", 0), ("V", 0), ("K", 1), ("V", 1), ("K", 2), ("V", 2), ("K", 3), ("V", 3), ("Q", 0),
         ("Q", 1), ("Q", 2), ("Q", 3)]
CHUNKS = [_first] + [_mixed] * (NB - 2) + [_last]
NCH = len(_mixed)
KQ = [[c for c in chunks if c[0] != "V"] for chunks in CHUNKS]
NKQ = len(KQ[0])


NS1 = -(-(TOP * (NB - 1) * TPB * P - N_EXPERTS * (P - 1)) // P)
NS2 = NS - NS1


def schedule():
    todo = []
    for b in range(NB):
        c, n, d = b - 1, b + 1, b - 2
        after = [
            [("lg", d, 3), ("gt", d, 0)],
            [("out", c, 0), ("gt", d, 1)],
            [("tr", c, 0), ("gt", d, 2)],
            [("wo", c, 0), ("out", c, 1), ("rt", d, 0)],
            [("nx", c, 0), ("tr", c, 1)],
            [("wo", c, 1), ("out", c, 2), ("xt", c, 0), ("en", d, 0)],
            [("nx", c, 1), ("tr", c, 2), ("lg", c, 0), ("en", d, 1)],
            [("wo", c, 2), ("out", c, 3), ("xt", c, 1), ("en", d, 2)],
            [("nx", c, 2), ("tr", c, 3), ("lg", c, 1), ("en", d, 3)],
            [("wo", c, 3), ("xt", c, 2), ("x", n, 0)],
            [("nx", c, 3), ("lg", c, 2), ("x", n, 1), ("x", n, 2)],
            [("xt", c, 3), ("x", n, 3)],
        ]
        for chunk, steps in zip(CHUNKS[b], after):
            todo.append((chunk[0], b, chunk[1]))
            kvs = {("K", 0): (c, 3), ("K", 1): (b, 0), ("K", 2): (b, 1), ("K", 3): (b, 2), ("Q", 0): (b, 3)}
            if chunk in kvs and kvs[chunk][0] >= 0 and not (chunk == ("Q", 0) and b < NB - 1):
                todo.append(("kv",) + kvs[chunk])
            todo += [s for s in steps if 0 <= s[1] < NB]
            if b == 0 and chunk == ("K", 1):
                todo.append(("wq_w", 0, 0))
            if b == 0 and chunk == ("Q", 1):
                todo.append(("wo_w", 0, 0))
            if b == 2 and chunk[0] == "Q":
                e, k = chunk[1] // 2, chunk[1] % 2 * 2
                todo += [(n, e, k + i) for i in range(2) for n in ("eh", "el")]
    c, d = NB - 1, NB - 2

    blocks = iter([(e, k) for e in range(2, 6) for k in range(4)])

    def we(n=1):
        return [(name,) + at for at in [next(blocks) for _ in range(n)] for name in ("eh", "el")]

    todo += [("lg", d, 3), ("out", c, 0), ("out", c, 1), ("tr", c, 0), ("gt", d, 0), ("tr", c, 1), ("wo", c, 0),
             ("gt", d, 1), ("out", c, 2), ("nx", c, 0), ("gt", d, 2), ("wo", c, 1), ("tr", c, 2), ("rt", d, 0),
             ("xt", c, 0), ("nx", c, 1), ("en", d, 0), ("out", c, 3), ("wo", c, 2), ("lg", c, 0), ("tr", c, 3),
             ("plan", 0, 0), ("xt", c, 1), ("nx", c, 2), ("en", d, 1), ("en", d, 2)] + we(2) + [
             ("wo", c, 3), ("lg", c, 1), ("en", d, 3), ("xt", c, 2)] + we(2) + [
             ("nx", c, 3), ("lg", c, 2)] + we(2) + [("xt", c, 3)] + we(2) + [("lg", c, 3)] + we(8)
    return todo


def build(nc, x, xT, wkT, wvT, wqT, woT, gateT, expert_w, expert_b, consts, no_entries, entries, out):
    C = x.shape[-1]
    KC = C // P
    NH, DH = 16, 32
    HG = P // DH
    E = N_EXPERTS
    GW = P + 2
    OW = P + HG
    EPS = 1e-5
    HIP, LOP = 0, 1
    RING = 4
    SLOTS_EARLY = 4
    FIRST = 16
    GATES_AT, PLACES_AT, PLAN_AT, GATE4_AT, TURN_AT, ENTER_AT = (0, 1, 2), 4, 5, 6, 7, 8
    TODO = schedule()
    assert x.shape[0] == N_TOKENS == NT * P and expert_w.shape[0] == E and KC == 4

    x1_rows = nc.dram_tensor("x1_rows", (N_TOKENS, C), F32, kind="Internal").ap()
    y_rows = nc.dram_tensor("y_rows", (TOP * N_TOKENS + TABLE, C), F32, kind="Internal").ap()
    table = nc.dram_tensor("table", (TABLE, ENTRY), I32, kind="Internal").ap()

    with ExitStack() as ctx:
        def sb(name, shape, dt=F32, stack=ctx):
            return stack.enter_context(nc.sbuf_tensor(name, shape, dt))

        def sem(name):
            return ctx.enter_context(nc.semaphore(name))

        acc = sb("acc", [P, NT, C])
        rowT_hi = sb("rowT_hi", [P, 2, KC, P], F32R)
        rowT_lo = sb("rowT_lo", [P, 2, KC, P], F32R)
        gate_raw = sb("gate_raw", [P, KC, E])
        gate_hl = sb("gate_hl", [P, KC, 2 * E], F32R)
        cst = sb("cst", [P, C_END])
        stats = sb("stats", [P, 6])
        mv = sb("mv", [P, 2, 2])
        var_eps = sb("var_eps", [P, 2])
        rstd = sb("rstd", [P, 2])
        nbias = sb("nbias", [P, 2])
        logit = sb("logit", [P, TPB, E])
        work = sb("work", [P, NT, E])
        at1 = sb("at1", [P, TPB, E])
        at2 = sb("at2", [P, TPB, E])
        one1 = sb("one1", [P, NT, E])
        one2 = sb("one2", [P, NT, E])
        chosen = sb("chosen", [P, NT, E])
        earlier = sb("earlier", [P, NT + 1, E])

        top1 = sb("top1", [P, TPB])
        top2 = sb("top2", [P, TPB])
        pick = sb("pick", [P, TOP, TPB])
        diff = sb("diff", [P, TPB])
        g1 = sb("g1", [P, TPB])
        g2 = sb("g2", [P, TPB])
        entry = sb("entry", [P, NT, TOP, ENTRY], I32)
        entry_at = sb("entry_at", [P, TOP, NT], I32)
        tiles_i = sb("tiles_i", [P, E], I32)
        tiles = sb("tiles", [P, E])
        first = sb("first", [P, E])
        skip = sb("skip", [P, E])
        taken = sb("taken", [P, E])
        before = sb("before", [P, E, E])
        is_past = sb("is_past", [1, NS2, E - 1])
        past_w = sb("past_w", [1, NS2, E - 1])
        plan_f = sb("plan_f", [1, 2, NS])
        plan = sb("plan", [1, 2, NS], I32)
        slot_in = sb("slot_in", [P, NS, ENTRY], I32)

        with ExitStack() as early:
            sb("experts01", [P, 2, 2, KC, C], F32, early)
            with ExitStack() as raws:
                w_hl = sb("w_hl", [P, 3, 2, KC, C], F32R, raws)
            w_raw = [sb(f"w{n}_raw", [P, 2, KC, C], F32, early) for n in "kvq"]
            xT_hi = sb("xT_hi", [P, KC, TPB * P], F32R, early)
            xT_lo = sb("xT_lo", [P, KC, TPB * P], F32R, early)
            with ExitStack() as raws:
                wo_hl = sb("wo_hl", [P, 2, KC, C], F32R, raws)
            wo_raw = sb("wo_raw", [P, 2, KC, C], F32, early)
            q_sb = sb("q_sb", [P, 2, KC, TPB * P], F32, early)
            x_raw = sb("x_raw", [P, TPB, KC, P], F32, early)
            k_sb = sb("k_sb", [P, 2, C], F32, early)
            v_sb = sb("v_sb", [P, 2, KC, GW], F32, early)
            exp_sb = sb("exp_sb", [P, 2, C], F32, early)
            kvbd = sb("kvbd", [P, KC, OW], F32, early)
            attn = sb("attn", [P, 2, C], F32, early)
            attnT_hi = sb("attnT_hi", [P, KC, P], F32R, early)
            attnT_lo = sb("attnT_lo", [P, KC, P], F32R, early)

            den = sb("den", [P, NH], F32, early)
            zden = sb("zden", [P, NH], F32, early)
        with ExitStack() as raws:
            y_in = sb("y_in", [P, NT, TOP, C], F32, raws)
        with ExitStack() as raws:
            ew = sb("ew", [P, E, 2, KC, C], F32R, raws)
        ew_raw = [sb(f"ew_raw{e}", [P, 2, KC, C]) for e in range(E)]
        rows = sb("rows", [P, RING, C])
        y_sb = sb("y_sb", [P, RING, C])
        bias_rows = sb("bias_rows", [P, C], F32R)
        bias_raw = sb("bias_raw", [P, C])
        bias_hi = sb("bias_hi", [P, C], F32R)
        bias_lo = sb("bias_lo", [P, C])
        gT = sb("gT", [P, NT // 4, P], F32R)
        gates = sb("gates", [P, NT, E])
        gate4 = sb("gate4", [P, NT, 4 * E], F32R)



        ident, minus_half = cst[:, COL["IDENT"]], cst[:, COL["HALF"]][:, 0:1]
        is_hi, is_lo = cst[:, COL["HI"]], cst[:, COL["LO"]]
        ones, tri = cst[:, COL["ONES"]], cst[:, COL["TRI"]]
        rank = cst[:, COL["RANK"]].rearrange("p (t e) -> p t e", e=E)
        ebase = cst[:, COL["EBASE"]].rearrange("p (t e) -> p t e", e=E)

        ps = ctx.enter_context(nc.psum_tensor("ps", [P, 8, C], F32))
        B_WO, B_KV, B_OUT, B_X1 = 2, 3, 5, 7
        kv_ps = ps[:, B_KV:B_KV + 2, 0:2 * GW].rearrange("p b (g n) -> p b g n", g=2)
        kvbd_v = kvbd[:, :, :].rearrange("p (b g) n -> p b g n", g=2)
        PLACE, COUNT = slice(64, 64 + TPB * E), slice(128, 128 + E)

        def place_bank(b):
            return B_KV if b >= NB - 2 else B_X1

        def bias_tiles(s):
            return range(2 * s - 2 * FIRST + NT, 2 * s - 2 * FIRST + NT + 2) if s >= FIRST - NT // 2 else range(0)

        def bias_bank(t):
            return 2 + t % 4

        def out_bank(m):
            return 0 if m >= NT - TPB and m % 2 else B_OUT

        def out_ps(m):
            b = out_bank(m)
            return ps[:, b:b + 2, 0:2 * OW].rearrange("p b (g n) -> p b g n", g=2)

        cst_in, gate_in, x_in, bias_in = sem("cst_in"), sem("gate_in"), sem("x_in"), sem("bias_in")
        w_in = [[sem(f"w{n}{k}_in") for k in range(KC)] for n in "kvqo"]
        xT_in = [sem(f"xT{i}_in") for i in range(TPB)]
        ew_in = [sem(f"ew{e}_in") for e in range(E)]
        x1_stored, table_emptied, scattered = sem("x1_stored"), sem("table_emptied"), sem("scattered")
        slot_in_done = [sem("slot_in0"), sem("slot_in1")]
        rows_in = [sem(f"rows_in{q}") for q in range(RING)]
        y_stored = [sem(f"y_stored{q}") for q in range(RING)]
        y_in_done = [sem(f"y_in{t}") for t in range(NT)]
        stored = sem("stored")
        zeroed = sem("zeroed")
        xT_hi_ready, xT_ready = sem("xT_hi_ready"), sem("xT_ready")
        w_hi_ready, w_ready = sem("w_hi_ready"), sem("w_ready")
        ew_hi_ready = sem("ew_hi_ready")
        ew_ready = sem("ew_ready")
        gate_hi_ready, gate_ready = sem("gate_hi_ready"), sem("gate_ready")
        proj_done, exp_done, kq_taken, kq_ready = sem("proj_done"), sem("exp_done"), sem("kq_taken"), sem("kq_ready")
        v_ready, kv_done, kvbd_ready = sem("v_ready"), sem("kv_done"), sem("kvbd_ready")
        out_done, den_ready, z_ready, attn_ready = sem("out_done"), sem("den_ready"), sem("z_ready"), sem("attn_ready")
        tr_done, attnT_hi_ready, attnT_ready = sem("tr_done"), sem("attnT_hi_ready"), sem("attnT_ready")
        wo_done, h_ready = sem("wo_done"), sem("h_ready")
        stats_ready, mv_ready, var_ready = sem("stats_ready"), sem("mv_ready"), sem("var_ready")
        rstd_ready, norm_ready, x1_ready = sem("rstd_ready"), sem("norm_ready"), sem("x1_ready")
        x1tr_done, x1T_hi_ready, x1T_ready = sem("x1tr_done"), sem("x1T_hi_ready"), sem("x1T_ready")
        logits_done, logits_read, step, diff_ready = sem("logits_done"), sem("logits_read"), sem("step"), sem("diff_ready")
        expd_ready, chosen_ready, place_done = sem("expd_ready"), sem("chosen_ready"), sem("place_done")
        place_read, entry_ready, plan_ready = sem("place_read"), sem("entry_ready"), sem("plan_ready")
        gate4_ready, gtr_done, gT_ready = sem("gate4_ready"), sem("gtr_done"), sem("gT_ready")
        rowtr_done, rowT_hi_ready, rowT_ready = sem("rowtr_done"), sem("rowT_hi_ready"), sem("rowT_ready")
        y_done, y_used = sem("y_done"), sem("y_used")
        bias_hi_ready, bias_ready, bias_done, bias_used = sem("bias_hi_ready"), sem("bias_ready"), sem("bias_done"), sem("bias_used")
        y_summed, y_added, y_out = sem("y_summed"), sem("y_added"), sem("y_out")

        ew_src = expert_w.rearrange("e (k p) o -> e p k o", p=P)

        def kq_number(b, kind, i):
            return KQ[b].index((kind, i)) + 1

        def projected(b, kind, i):
            return NCH * b + CHUNKS[b].index((kind, i)) + 1

        def at_least(eng, semaphore, value):
            if value > 0:
                eng.wait_ge(semaphore, value)

        def expert_low(eng, ops, e, k):
            eng.wait_ge(ew_hi_ready, e * KC + k + 1)
            if k == 0 and e in (2, E - 1):
                eng.wait_ge(ew_ready, e * KC)
            ops.tensor_tensor(ew[:, e, LOP, k, :], ew_raw[e][:, LOP, k, :], ew[:, e, HIP, k, :].bitcast(F32),
                              ALU.subtract).then_inc(ew_ready, 1)

        block = ctx.enter_context(nc.Block())

        @block.sync
        def _(sp):
            def load_xT(b, i):
                at_least(sp, xT_ready, TPB * (b - 1) + i + 1 if b else 0)
                sp.dma_start(x_raw[:, i, :, :], xT[TPB * b + i].rearrange("p (k t) -> p k t", k=KC))\
                    .then_inc(xT_in[i], 16)

            def load_w(m, src, dst):
                for k in range(KC):
                    sp.dma_start(dst[:, k, :], src[:, k, :]).then_inc(w_in[m][k], 16)

            def load_expert(e):
                sp.dma_start(ew_raw[e][:, LOP], ew_src[e]).then_inc(ew_in[e], 16)

            def load_slots(s, q):
                if not isinstance(s, int) or s >= 2:
                    sp.wait_ge(slot_in_done[q], (s - q) * 8)
                row = sp.value_load(plan[0:1, 1, s:s + 1] if isinstance(s, int) else plan[0:1, 1, ds(s, 1)],
                                    min_val=0, max_val=TABLE - P)
                sp.dma_start(slot_in[:, s, :] if isinstance(s, int) else slot_in[:, ds(s, 1), :],
                             table[ds(row, P), :]).then_inc(slot_in_done[q], 16)

            load_xT(0, 0)
            load_w(0, wkT, w_raw[0][:, LOP])
            load_w(1, wvT, w_raw[1][:, LOP])
            for i in range(1, TPB):
                load_xT(0, i)
            load_w(2, wqT, w_raw[2][:, LOP])
            load_w(3, woT, wo_raw[:, LOP])
            sp.dma_start(acc[:, :, :], x.rearrange("(t p) c -> p t c", p=P)).then_inc(x_in, 16)
            sp.dma_start(table, no_entries).then_inc(table_emptied, 16)
            load_expert(0)
            load_expert(1)
            for name, b, i in TODO:
                if name == "x":
                    load_xT(b, i)
                if name == "nx":
                    m = TPB * b + i
                    sp.wait_ge(x1_ready, m + 1)
                    sp.dma_start(x1_rows[m * P:(m + 1) * P, :], acc[:, m, :]).then_inc(x1_stored, 16)
                if (name, b, i) == ("nx", NB - 1, 3):
                    sp.wait_ge(plan_ready, 1)
                    sp.wait_ge(scattered, 16 * TOP * (NT - TPB))
                    for s in range(SLOTS_EARLY):
                        load_slots(s, s % 2)
                if (name, b, i) == ("lg", NB - 1, 1):
                    sp.wait_ge(wo_done, NT)
                    load_expert(6)
                    load_expert(7)
                if b == NB - 1 and (name, i) in (("V", 3), ("Q", 3)):
                    sp.wait_ge(proj_done, projected(b, name, i))
                    for e in (2, 3) if name == "V" else (4, 5):
                        load_expert(e)
            for r in range(P // E):
                sp.dma_start(bias_raw[r * E:(r + 1) * E, :], expert_b).then_inc(bias_in, 16)
            load_slots(SLOTS_EARLY, 0)
            load_slots(SLOTS_EARLY + 1, 1)
            with sp.Fori(SLOTS_EARLY // 2 + 1, NS1 // 2) as j:
                for q in range(2):
                    load_slots(2 * j + q, q)
            load_slots(NS1 - 1, 0)
            sp.wait_ge(plan_ready, 2)
            sp.wait_ge(scattered, 16 * TOP * NT)
            load_slots(NS1, 1)
            with sp.Fori(NS1 // 2 + 1, NS // 2) as j:
                for q in range(2):
                    load_slots(2 * j + q, q)
            load_slots(NS - 1, 0)
            sp.wait_ge(ew_ready, E * KC)
            sp.wait_ge(y_used, NS)
            for q in range(RING):
                sp.wait_ge(y_stored[q], 16 * ((NS - q + RING - 1) // RING))
            for t in range(NT):
                sp.dma_start(y_in[:, t, :, :], y_rows[TOP * t * P:TOP * (t + 1) * P, :]
                             .rearrange("(p c) n -> p c n", c=TOP)).then_inc(y_in_done[t], 16)
            for t in range(NT):
                sp.wait_ge(y_out, t + 1)
                sp.dma_start(out[t * P:(t + 1) * P, :], acc[:, t, :]).then_inc(stored, 16)
            sp.wait_ge(stored, 16 * NT)

        @block.gpsimd
        def _(pool):
            pool.dma_start(cst[:, :], consts).then_inc(cst_in, 16)
            pool.dma_start(gate_raw[:, :, :], gateT).then_inc(gate_in, 16)
            pool.dma_start(entry[:, :, :, :], entries).then_inc(gate_in, 16)
            nc.gpsimd.memset(kvbd[:, :, :], 0.0).then_inc(zeroed, 1)
            nc.gpsimd.memset(v_sb[:, :, :, :], 1.0).then_inc(zeroed, 1)

            def power(n):
                pool.wait_ge(var_ready, n + 1)
                nc.gpsimd.tensor_tensor(rstd[:, n % 2:n % 2 + 1], var_eps[:, n % 2:n % 2 + 1], minus_half, ALU.pow).then_inc(rstd_ready, 1)

            def enter(t):
                pool.wait_ge(entry_ready, t // TPB + 1)
                for c in range(TOP):
                    pool.indirect_dma_start(
                        out=table, out_offset=bass.IndirectOffsetOnAxis(ap=entry_at[:, c, t:t + 1], axis=0),
                        in_=entry[:, t, c, :], in_offset=None).then_inc(scattered, 16)

            pool.wait_ge(cst_in, 16)
            pool.wait_ge(table_emptied, 16)
            for name, b, i in TODO:
                if name == "wo":
                    power(TPB * b + i)
                if name == "en":
                    enter(TPB * b + i)
                if name == "el" and b < 2:
                    expert_low(pool, nc.gpsimd, b, i)
            pool.wait_ge(x1_stored, 16 * NT)
            LATER = 4
            for s in range(NS + LATER):
                if s == LATER:
                    for k in range(KC):
                        expert_low(pool, nc.gpsimd, E - 1, k)
                if s >= ENTER_AT and s < ENTER_AT + TPB:
                    if s == ENTER_AT:
                        pool.wait_ge(slot_in_done[0], 16 * ((NS1 + 1) // 2))
                        pool.wait_ge(slot_in_done[1], 16 * (NS1 // 2))
                    enter(NT - TPB + s - ENTER_AT)
                if s < NS:
                    pool.wait_ge(slot_in_done[s % 2], 16 * (s // 2 + 1))
                    at_least(pool, rowtr_done, s - RING + 1)
                    pool.indirect_dma_start(
                        out=rows[:, s % RING, :], out_offset=None, in_=x1_rows,
                        in_offset=bass.IndirectOffsetOnAxis(ap=slot_in[:, s, 0:1], axis=0))\
                        .then_inc(rows_in[s % RING], 16)
                if s >= LATER:
                    z = s - LATER
                    pool.wait_ge(y_used, z + 1)
                    pool.indirect_dma_start(
                        out=y_rows, out_offset=bass.IndirectOffsetOnAxis(ap=slot_in[:, z, 2:3], axis=0),
                        in_=y_sb[:, z % RING, :], in_offset=None).then_inc(y_stored[z % RING], 16)
            for t in range(NT + 2):
                if t < NT:
                    pool.wait_ge(y_in_done[t], 16)
                    nc.gpsimd.tensor_tensor(y_in[:, t, 0, :], y_in[:, t, 0, :], y_in[:, t, 1, :], ALU.add)\
                        .then_inc(y_summed, 1)
                if t >= 2:
                    power(NT + t - 2)

        @block.scalar
        def _(act):
            def split_x(b, i):
                tok = slice(i * P, (i + 1) * P)
                act.wait_ge(xT_in[i], 16 * b + 16)
                if b:
                    act.wait_ge(proj_done, projected(b - 1, *(("Q", 3) if i < 3 else ("V", 3))))
                nc.scalar.copy(xT_hi[:, :, tok], x_raw[:, i, :, :]).then_inc(xT_hi_ready, 1)

            def split_w(m, hl, raw):
                for k in range(KC):
                    act.wait_ge(w_in[m][k], 16)
                    nc.scalar.copy(hl[:, HIP, k, :], raw[:, LOP, k, :]).then_inc(w_hi_ready, 1)

            def expert_high(e, k):
                act.wait_ge(ew_in[e], 16)
                nc.scalar.copy(ew[:, e, HIP, k, :], ew_raw[e][:, LOP, k, :]).then_inc(ew_hi_ready, 1)

            def exp_of(b, kind, i):
                at, n = CHUNKS[b].index((kind, i)), kq_number(b, kind, i)
                act.wait_ge(proj_done, projected(b, kind, i))
                at_least(act, kq_ready, NKQ * b + n - 2)
                nc.scalar.activation(exp_sb[:, n % 2, :], ps[:, at % 2, :], ACT.Exp).then_inc(exp_done, 1)

            def take_v(b, i):
                at = CHUNKS[b].index(("V", i))
                act.wait_ge(proj_done, projected(b, "V", i))
                act.wait_ge(zeroed, 2)
                at_least(act, kv_done, TPB * b + i - 1)
                nc.scalar.copy(v_sb[:, i % 2, :, 0:P],
                               ps[:, at % 2, :].rearrange("p (g n) -> p g n", g=KC)).then_inc(v_ready, 1)

            def normalise(n, m, ready):
                act.wait_ge(norm_ready, n + 1)
                nc.scalar.activation(acc[:, m, :], acc[:, m, :], ACT.Identity, bias=nbias[:, n % 2:n % 2 + 1],
                                     scale=rstd[:, n % 2:n % 2 + 1]).then_inc(ready, 1)

            def exp_gate(b):
                act.wait_ge(diff_ready, b + 1)
                nc.scalar.activation(g2[:, :], diff[:, :], ACT.Exp).then_inc(expd_ready, 1)

            def attnT_high(m):
                act.wait_ge(tr_done, m + 1)
                at_least(act, wo_done, m)
                nc.scalar.copy(attnT_hi[:, :, :], ps[:, out_bank(m), :].rearrange("p (k t) -> p k t", k=KC))\
                    .then_inc(attnT_hi_ready, 1)

            split_x(0, 0)
            split_w(0, w_hl[:, 0], w_raw[0])
            split_w(1, w_hl[:, 1], w_raw[1])
            for i in range(1, TPB):
                split_x(0, i)
            for name, b, i in TODO:
                m = TPB * b + i
                if name in ("K", "Q"):
                    exp_of(b, name, i)
                elif name == "V":
                    take_v(b, i)
                elif name == "wq_w":
                    split_w(2, w_hl[:, 2], w_raw[2])
                elif name == "wo_w":
                    split_w(3, wo_hl, wo_raw)
                    act.wait_ge(gate_in, 32)
                    nc.scalar.copy(gate_hl[:, :, 0:E], gate_raw[:, :, :]).then_inc(gate_hi_ready, 1)
                elif name == "x":
                    split_x(b, i)
                elif name == "eh":
                    expert_high(b, i)
                elif name == "tr":
                    attnT_high(m)
                elif name == "nx":
                    normalise(m, m, x1_ready)
                elif name == "xt":
                    act.wait_ge(x1tr_done, m + 1)
                    at_least(act, logits_done, m - 1)
                    nc.scalar.copy(rowT_hi[:, m % 2, :, :], ps[:, B_X1, :].rearrange("p (k t) -> p k t", k=KC))\
                        .then_inc(x1T_hi_ready, 1)
                elif name == "gt" and i == 1:
                    exp_gate(b)
            def row_high(s, q):
                act.wait_ge(rowtr_done, s + 1)
                if not isinstance(s, int) or s >= 2:
                    act.wait_ge(y_done, s - 1)
                nc.scalar.copy(rowT_hi[:, q, :, :], ps[:, 6 + q, :].rearrange("p (k t) -> p k t", k=KC))\
                    .then_inc(rowT_hi_ready, 1)

            for s in range(FIRST):
                if s < 2:
                    act.wait_ge(logits_done, NT - 1 + s)
                row_high(s, s % 2)
                if s == 1:
                    for e in range(6, E):
                        for k in range(KC):
                            expert_high(e, k)
                if s == GATES_AT[1] + 1:
                    exp_gate(NB - 1)
                if s == GATE4_AT:
                    act.wait_ge(bias_in, 16 * (P // E))
                    nc.scalar.copy(bias_hi[:, :], bias_raw[:, :]).then_inc(bias_hi_ready, 1)
                if s == TURN_AT + 1:
                    act.wait_ge(gtr_done, 1)
                    nc.scalar.copy(gT[:, :, :], ps[:, 5, :].rearrange("p (q t) -> p q t", q=NT // 4))\
                        .then_inc(gT_ready, 1)
            with act.Fori(FIRST // RING, NS // RING) as j:
                for q in range(RING):
                    row_high(RING * j + q, q % 2)
            for s in range(NS // RING * RING, NS):
                row_high(s, s % 2)
            for t in range(NT):
                normalise(NT + t, t, y_out)

        @block.vector
        def _(dve):
            steps = [0]

            def link(ins):
                steps[0] += 1
                ins.then_inc(step, 1)
                dve.wait_ge(step, steps[0])

            def split_x(b, i):
                tok = slice(i * P, (i + 1) * P)
                dve.wait_ge(xT_hi_ready, TPB * b + i + 1)
                nc.vector.tensor_tensor(xT_lo[:, :, tok], x_raw[:, i, :, :], xT_hi[:, :, tok].bitcast(F32),
                                        ALU.subtract).then_inc(xT_ready, 1)

            def split_w(m, hl, raw):
                for k in range(KC):
                    dve.wait_ge(w_hi_ready, m * KC + k + 1)
                    nc.vector.tensor_tensor(hl[:, LOP, k, :], raw[:, LOP, k, :], hl[:, HIP, k, :].bitcast(F32),
                                            ALU.subtract).then_inc(w_ready, 1)

            def feature_map(b, kind, i):
                at, n = CHUNKS[b].index((kind, i)), kq_number(b, kind, i)
                if kind == "K":
                    dst = k_sb[:, i % 2, :]
                    at_least(dve, kv_done, TPB * b + i - 1)
                else:
                    dst = q_sb[:, b % 2, i, :]
                    at_least(dve, out_done, TPB * (b - 1))
                dve.wait_ge(exp_done, NKQ * b + n)
                nc.vector.tensor_scalar(dst, ps[:, at % 2, :], 0.0, None, ALU.max).then_inc(kq_taken, 1)
                dve.wait_ge(kq_taken, NKQ * b + n)
                nc.vector.scalar_tensor_tensor(out=dst, in0=exp_sb[:, n % 2, :], scalar=1.0, in1=dst,
                                               op0=ALU.min, op1=ALU.add).then_inc(kq_ready, 1)

            def take_kv(b):
                dve.wait_ge(kv_done, TPB * b + TPB)
                dve.wait_ge(zeroed, 2)
                at_least(dve, out_done, TPB * b)
                for j in range(HG):
                    h = slice(j * DH, (j + 1) * DH)
                    nc.vector.tensor_copy(kvbd_v[h, :, :, h], kv_ps[h, :, :, h]).then_inc(kvbd_ready, 1)
                    nc.vector.tensor_copy(kvbd_v[h, :, :, P + j:P + j + 1], kv_ps[h, :, :, P:P + 1])\
                        .then_inc(kvbd_ready, 1)

            def take_out(m):
                src = out_ps(m)
                dve.wait_ge(out_done, m + 1)
                nc.vector.tensor_scalar(den[:, :].rearrange("p (b g h) -> p b g h", b=2, g=2),
                                        src[:, :, :, P:OW], 1e-6, None, ALU.add).then_inc(den_ready, 1)
                dve.wait_ge(den_ready, m + 1)
                nc.vector.reciprocal(zden[:, :], den[:, :]).then_inc(z_ready, 1)
                dve.wait_ge(z_ready, m + 1)
                at_least(dve, tr_done, m - 1)
                for c in range(2):
                    half = slice(c * 2 * P, (c + 1) * 2 * P)
                    nc.vector.tensor_tensor(
                        attn[:, m % 2, half].rearrange("p (g h e) -> p g h e", g=2, h=HG),
                        src[:, c, :, 0:P].rearrange("p g (h e) -> p g h e", h=HG),
                        zden[:, c * 8:c * 8 + 8].rearrange("p (g h) -> p g h", g=2).unsqueeze(3)
                        .to_broadcast([P, 2, HG, DH]), ALU.mult).then_inc(attn_ready, 1)

            def attnT_low(m):
                dve.wait_ge(attnT_hi_ready, m + 1)
                nc.vector.tensor_tensor(attnT_lo[:, :, :], ps[:, out_bank(m), :].rearrange("p (k t) -> p k t", k=KC),
                                        attnT_hi[:, :, :].bitcast(F32), ALU.subtract).then_inc(attnT_ready, 1)

            def statistics(n, a):
                q = n % 2
                nc.vector.bn_stats(stats[:, :], a).then_inc(stats_ready, 1)
                dve.wait_ge(stats_ready, n + 1)
                nc.vector.bn_aggr(mv[:, q, :], stats[:, :]).then_inc(mv_ready, 1)
                dve.wait_ge(mv_ready, n + 1)
                nc.vector.tensor_scalar(var_eps[:, q:q + 1], mv[:, q, 1:2], EPS, None, ALU.add).then_inc(var_ready, 1)

            def norm_bias(n):
                q = n % 2
                dve.wait_ge(rstd_ready, n + 1)
                nc.vector.tensor_scalar(nbias[:, q:q + 1], mv[:, q, 0:1], rstd[:, q:q + 1], -1.0, ALU.mult, ALU.mult)\
                    .then_inc(norm_ready, 1)

            def take_wo(m):
                dve.wait_ge(wo_done, m + 1)
                a = acc[:, m, :]
                nc.vector.tensor_tensor(a, ps[:, B_WO, :], a, ALU.add).then_inc(h_ready, 1)
                dve.wait_ge(h_ready, m + 1)
                at_least(dve, x1_ready, m - 1)
                statistics(m, a)

            def argmax(w, one, top, p):
                like = [P, TPB, E]
                link(nc.vector.tensor_reduce(top, w, AX_X, ALU.max))
                link(nc.vector.tensor_tensor(one, w, top.unsqueeze(2).to_broadcast(like), ALU.is_equal))
                link(nc.vector.tensor_tensor(one, one, rank, ALU.mult))
                link(nc.vector.tensor_reduce(p, one, AX_X, ALU.max))
                link(nc.vector.tensor_tensor(one, one, p.unsqueeze(2).to_broadcast(like), ALU.is_equal))

            def choose(b, part):
                lo, hi = TPB * b, TPB * b + TPB
                at = slice(lo, hi)
                w, o1, o2, p, t1, t2 = work[:, 0:TPB, :], one1[:, at, :], one2[:, at, :], pick[:, 0, :], top1[:, :], top2[:, :]
                if part == 0:
                    dve.wait_ge(logits_read, hi)
                    argmax(logit[:, :, :], o1, t1, p)
                elif part == 1:
                    link(nc.vector.tensor_scalar(w, o1, -3.0e38, None, ALU.mult))
                    link(nc.vector.tensor_tensor(w, w, logit[:, :, :], ALU.add))
                    argmax(w, o2, t2, p)
                    nc.vector.tensor_tensor(diff[:, :], t2, t1, ALU.subtract).then_inc(diff_ready, 1)
                else:
                    nc.vector.tensor_tensor(chosen[:, at, :], o1, o2, ALU.add).then_inc(chosen_ready, 1)
                    dve.wait_ge(chosen_ready, lo + b + 1)
                    for t in range(lo, hi):
                        nc.vector.tensor_tensor(earlier[:, t + 1, :], earlier[:, t, :], chosen[:, t, :], ALU.add)\
                            .then_inc(chosen_ready, 1)
                        dve.wait_ge(chosen_ready, t + b + 2)
                    dve.wait_ge(expd_ready, b + 1)
                    a, z = g1[:, :], g2[:, :]
                    link(nc.vector.tensor_scalar(a, z, 1.0, None, ALU.add))
                    link(nc.vector.reciprocal(a, a))
                    nc.vector.tensor_copy(entry[:, at, 0, 1].bitcast(F32), a)
                    link(nc.vector.tensor_tensor(entry[:, at, 1, 1].bitcast(F32), z, a, ALU.mult))

            def enter(b):
                at = slice(TPB * b, TPB * b + TPB)
                dve.wait_ge(place_done, b + 1)
                nc.vector.tensor_tensor(work[:, 0:TPB, :], ps[:, place_bank(b), PLACE]
                                        .rearrange("p (t e) -> p t e", e=E), ebase, ALU.add)\
                    .then_inc(place_read, 1)
                dve.wait_ge(place_read, b + 1)
                nc.vector.tensor_tensor(at1[:, :, :], work[:, 0:TPB, :], one1[:, at, :], ALU.mult)
                link(nc.vector.tensor_tensor(at2[:, :, :], work[:, 0:TPB, :], one2[:, at, :], ALU.mult))
                nc.vector.tensor_reduce(pick[:, 0, :], at1[:, :, :], AX_X, ALU.add)
                link(nc.vector.tensor_reduce(pick[:, 1, :], at2[:, :, :], AX_X, ALU.add))
                nc.vector.tensor_copy(entry_at[:, :, at], pick[:, :, :]).then_inc(entry_ready, 1)

            def make_plan(part):
                n, at = (NS1, slice(0, NS1)) if part == 0 else (NS2, slice(NS1, NS))
                past, w = is_past[:, 0:n, :], past_w[:, 0:n, :]
                link(nc.vector.tensor_scalar(tiles_i[:, :], ps[:, B_KV, COUNT], float((P - 1) * part), None, ALU.add))
                link(nc.vector.tensor_scalar(tiles_i[:, :], tiles_i[:, :], P.bit_length() - 1, None,
                                             ALU.logical_shift_right))
                link(nc.vector.tensor_copy(tiles[:, :], tiles_i[:, :]))
                if part == 1:
                    link(nc.vector.tensor_tensor(tiles[:, :], tiles[:, :], taken[:, :], ALU.subtract))
                link(nc.vector.tensor_tensor(before[:, :, :], tiles[:, :].unsqueeze(1).to_broadcast([P, E, E]),
                                             cst[:, COL["BEFORE"]].rearrange("p (e f) -> p e f", f=E), ALU.mult))
                link(nc.vector.tensor_reduce(first[:, :], before[:, :, :], AX_X, ALU.add))
                link(nc.vector.tensor_tensor(
                    past, cst[0:1, COL["SLOT"]][:, 0:n].unsqueeze(2).to_broadcast([1, n, E - 1]),
                    first[0:1, 1:E].unsqueeze(1).to_broadcast([1, n, E - 1]), ALU.is_ge))
                if part == 1:
                    link(nc.vector.tensor_tensor(tiles[:, :], tiles[:, :], taken[:, :], ALU.add))
                    link(nc.vector.tensor_tensor(tiles[:, 0:E - 1], tiles[:, 0:E - 1], taken[:, 1:E], ALU.subtract))
                link(nc.vector.tensor_scalar(skip[:, :], tiles[:, :], -float(P), float(REGION), ALU.mult, ALU.add))
                link(nc.vector.tensor_tensor(w, past, skip[0:1, 0:E - 1].unsqueeze(1).to_broadcast([1, n, E - 1]),
                                             ALU.mult))
                nc.vector.tensor_reduce(plan_f[:, 0, at], past, AX_X, ALU.add)
                link(nc.vector.tensor_reduce(plan_f[:, 1, at], w, AX_X, ALU.add))
                link(nc.vector.tensor_tensor(plan_f[:, 1, at], plan_f[:, 1, at], cst[0:1, COL["SLOTROW"]][:, 0:n],
                                             ALU.add))
                if part == 1:
                    link(nc.vector.tensor_scalar(skip[:, 0:1], taken[:, 0:1], float(P), None, ALU.mult))
                    link(nc.vector.tensor_scalar(plan_f[:, 1, at], plan_f[:, 1, at], skip[0:1, 0:1], None, ALU.add))
                nc.vector.tensor_copy(plan[:, :, at], plan_f[:, :, at]).then_inc(plan_ready, 1)
                if part == 0:
                    link(nc.vector.tensor_scalar(taken[:, :], first[:, :], -1.0, float(NS1), ALU.mult, ALU.add))
                    link(nc.vector.tensor_scalar(taken[:, :], taken[:, :], 0.0, None, ALU.max))
                    link(nc.vector.tensor_tensor(taken[:, :], taken[:, :], tiles[:, :], ALU.min))

            dve.wait_ge(cst_in, 16)
            link(nc.vector.memset(earlier[:, 0, :], 0.0))
            split_x(0, 0)
            split_w(0, w_hl[:, 0], w_raw[0])
            split_w(1, w_hl[:, 1], w_raw[1])
            for i in range(1, TPB):
                split_x(0, i)
            for name, b, i in TODO:
                m = TPB * b + i
                if name in ("K", "Q"):
                    feature_map(b, name, i)
                elif name == "wq_w":
                    split_w(2, w_hl[:, 2], w_raw[2])
                elif name == "wo_w":
                    split_w(3, wo_hl, wo_raw)
                    dve.wait_ge(gate_hi_ready, 1)
                    nc.vector.tensor_tensor(gate_hl[:, :, E:2 * E], gate_raw[:, :, :],
                                            gate_hl[:, :, 0:E].bitcast(F32), ALU.subtract).then_inc(gate_ready, 1)
                elif name == "x":
                    split_x(b, i)
                elif name == "kv" and i == TPB - 1:
                    take_kv(b)
                elif name == "out":
                    take_out(m)
                elif name == "tr":
                    attnT_low(m)
                elif name == "wo":
                    if m == 0:
                        dve.wait_ge(x_in, 16)
                    take_wo(m)
                elif name == "nx":
                    norm_bias(m)
                elif name == "xt":
                    dve.wait_ge(x1T_hi_ready, m + 1)
                    nc.vector.tensor_tensor(rowT_lo[:, m % 2, :, :], ps[:, B_X1, :].rearrange("p (k t) -> p k t", k=KC),
                                            rowT_hi[:, m % 2, :, :].bitcast(F32), ALU.subtract).then_inc(x1T_ready, 1)
                elif name == "lg":
                    dve.wait_ge(logits_done, m + 1)
                    nc.vector.tensor_reduce(logit[:, i, :], ps[:, B_X1, 0:2 * E].rearrange("p (a e) -> p e a", a=2),
                                            AX_X, ALU.add).then_inc(logits_read, 1)
                elif name == "el" and b >= 2:
                    expert_low(dve, nc.vector, b, i)
                elif name == "plan":
                    make_plan(0)
                elif name == "gt":
                    choose(b, i)
                elif name == "rt":
                    enter(b)


            def row_low(s, q):
                dve.wait_ge(rowT_hi_ready, s + 1)
                nc.vector.tensor_tensor(rowT_lo[:, q, :, :], ps[:, 6 + q, :].rearrange("p (k t) -> p k t", k=KC),
                                        rowT_hi[:, q, :, :].bitcast(F32), ALU.subtract).then_inc(rowT_ready, 1)

            def take_y(s, q, nth):
                dve.wait_ge(y_done, s + 1)
                if not isinstance(s, int) or s >= RING:
                    dve.wait_ge(y_stored[q], 16 * nth)
                gate = slot_in[:, s, 1:2] if isinstance(s, int) else slot_in[:, ds(s, 1), 1]
                nc.vector.tensor_scalar(y_sb[:, q, :], ps[:, q % 2, :], gate.bitcast(F32), None, ALU.mult)\
                    .then_inc(y_used, 1)

            def gates_and_biases():
                gate_of = entry[:, :, :, 1].bitcast(F32)
                for c, one in enumerate((one1, one2)):
                    to = work if c == 0 else gates
                    link(nc.vector.tensor_tensor(to[:, :, :], one[:, :, :],
                                                 gate_of[:, :, c].unsqueeze(2).to_broadcast([P, NT, E]), ALU.mult))
                link(nc.vector.tensor_tensor(gates[:, :, :], gates[:, :, :], work[:, :, :], ALU.add))
                link(nc.vector.tensor_copy(gate4[:, :, 0:E], gates[:, :, :]))
                nc.vector.tensor_copy(gate4[:, :, E:2 * E], gates[:, :, :]).then_inc(gate4_ready, 1)
                for q in (2, 3):
                    nc.vector.tensor_tensor(gate4[:, :, q * E:(q + 1) * E], gates[:, :, :],
                                            gate4[:, :, 0:E].bitcast(F32), ALU.subtract).then_inc(gate4_ready, 1)
                dve.wait_ge(bias_hi_ready, 1)
                link(nc.vector.tensor_tensor(bias_lo[:, :], bias_raw[:, :], bias_hi[:, :].bitcast(F32), ALU.subtract))
                link(nc.vector.tensor_scalar(bias_rows[:, :], bias_lo[:, :], is_lo, None, ALU.mult))
                nc.vector.scalar_tensor_tensor(out=bias_rows[:, :], in0=bias_hi[:, :].bitcast(F32), scalar=is_hi,
                                               in1=bias_rows[:, :].bitcast(F32), op0=ALU.mult, op1=ALU.add)\
                    .then_inc(bias_ready, 1)

            row_low(0, 0)
            row_low(1, 1)
            for k in range(KC):
                expert_low(dve, nc.vector, E - 2, k)
            for s in range(FIRST):
                if s:
                    row_low(s + 1, (s + 1) % 2)
                take_y(s, s % RING, s // RING)
                if s in GATES_AT:
                    choose(NB - 1, s)
                if s == PLACES_AT:
                    enter(NB - 1)
                if s == PLAN_AT:
                    make_plan(1)
                if s == GATE4_AT:
                    gates_and_biases()
                for t in bias_tiles(s):
                    if t == 0:
                        dve.wait_ge(x1_stored, 16 * NT)
                    dve.wait_ge(bias_done, t + 1)
                    nc.vector.tensor_tensor(acc[:, t, :], ps[:, bias_bank(t), :], acc[:, t, :], ALU.add)\
                        .then_inc(bias_used, 1)
            with dve.Fori(FIRST // RING, NS // RING) as j:
                for q in range(RING):
                    row_low(RING * j + (q + 1), (q + 1) % 2)
                    take_y(RING * j + q, q, j)
            for s in range(NS // RING * RING, NS):
                if s + 1 < NS:
                    row_low(s + 1, (s + 1) % 2)
                take_y(s, s % RING, s // RING)
            def add_outputs(t):
                dve.wait_ge(y_summed, t + 1)
                nc.vector.tensor_tensor(acc[:, t, :], acc[:, t, :], y_in[:, t, 0, :], ALU.add).then_inc(y_added, 1)

            dve.wait_ge(x1_ready, NT)
            add_outputs(0)
            for t in range(NT):
                n, q = NT + t, t % 2
                dve.wait_ge(y_added, t + 1)
                nc.vector.bn_stats(stats[:, :], acc[:, t, :]).then_inc(stats_ready, 1)
                if t + 1 < NT:
                    add_outputs(t + 1)
                dve.wait_ge(stats_ready, n + 1)
                at_least(dve, y_out, t - 1)
                nc.vector.bn_aggr(mv[:, q, :], stats[:, :]).then_inc(mv_ready, 1)
                if t:
                    norm_bias(n - 1)
                dve.wait_ge(mv_ready, n + 1)
                nc.vector.tensor_scalar(var_eps[:, q:q + 1], mv[:, q, 1:2], EPS, None, ALU.add).then_inc(var_ready, 1)
            norm_bias(2 * NT - 1)

        @block.tensor
        def _(pe):
            def three(bank, lhs_hi, lhs_lo, rhs_hi, rhs_lo, arrived=None):
                for k in range(KC):
                    if arrived is not None:
                        pe.wait_ge(w_ready, arrived + k + 1)
                    nc.tensor.matmul(bank, lhs_hi(k), rhs_hi(k), start=(k == 0), stop=False)
                    nc.tensor.matmul(bank, lhs_hi(k), rhs_lo(k), start=False, stop=False)
                    last = nc.tensor.matmul(bank, lhs_lo(k), rhs_hi(k), start=False, stop=(k == KC - 1))
                return last

            def project(b, kind, i):
                at, w = CHUNKS[b].index((kind, i)), "KVQ".index(kind)
                pe.wait_ge(xT_ready, TPB * b + (TPB if kind == "Q" else i + 1))
                if b or at >= 2:
                    bb = b - (at < 2)
                    back = CHUNKS[bb][(at - 2) % NCH]
                    if back[0] == "V":
                        pe.wait_ge(v_ready, TPB * bb + back[1] + 1)
                    else:
                        pe.wait_ge(kq_taken, NKQ * bb + kq_number(bb, *back))
                bank, arrived = ps[:, at % 2, :], w * KC if b == 0 and i == 0 else None
                here = slice(i * P, (i + 1) * P)
                if kind == "Q":
                    last = three(bank, lambda k: w_hl[:, w, HIP, k, here], lambda k: w_hl[:, w, LOP, k, here],
                                 lambda k: xT_hi[:, k, :], lambda k: xT_lo[:, k, :], arrived)
                else:
                    last = three(bank, lambda k: xT_hi[:, k, here], lambda k: xT_lo[:, k, here],
                                 lambda k: w_hl[:, w, HIP, k, :], lambda k: w_hl[:, w, LOP, k, :], arrived)
                last.then_inc(proj_done, 1)

            def kv(b, i):
                pe.wait_ge(kq_ready, NKQ * b + kq_number(b, "K", i))
                pe.wait_ge(v_ready, TPB * b + i + 1)
                if i == 0:
                    at_least(pe, kvbd_ready, 2 * HG * b)
                for g in range(KC):
                    last = nc.tensor.matmul(kv_ps[:, g // 2, g % 2, :], k_sb[:, i % 2, g * P:(g + 1) * P],
                                            v_sb[:, i % 2, g, :], start=(i == 0 and g % 2 == 0), stop=(i == TPB - 1),
                                            skip_group_check=True)
                last.then_inc(kv_done, 1)

            def attend(b, m, i):
                dst = out_ps(m)
                pe.wait_ge(kq_ready, NKQ * b + kq_number(b, "Q", 3))
                pe.wait_ge(kvbd_ready, 2 * HG * b + 2 * HG)
                if out_bank(m) == out_bank(m - 1):
                    at_least(pe, attnT_ready, m)
                    at_least(pe, attn_ready, 2 * m)
                elif m == NT - TPB + 1:
                    pe.wait_ge(v_ready, NT)
                    pe.wait_ge(kq_taken, NKQ * NB)
                else:
                    pe.wait_ge(attnT_ready, m - 1)
                    pe.wait_ge(attn_ready, 2 * m - 2)
                for g in range(KC):
                    last = nc.tensor.matmul(dst[:, g // 2, g % 2, :], q_sb[:, b % 2, g, i * P:(i + 1) * P],
                                            kvbd[:, g, :], start=True, stop=True)
                last.then_inc(out_done, 1)

            def turn(m):
                pe.wait_ge(attn_ready, 2 * m + 2)
                for k in range(KC):
                    last = nc.tensor.transpose(ps[:, out_bank(m), k * P:(k + 1) * P],
                                               attn[:, m % 2, k * P:(k + 1) * P], ident)
                last.then_inc(tr_done, 1)

            def output(m):
                pe.wait_ge(attnT_ready, m + 1)
                at_least(pe, h_ready, m)
                three(ps[:, B_WO, :], lambda k: attnT_hi[:, k, :], lambda k: attnT_lo[:, k, :],
                      lambda k: wo_hl[:, HIP, k, :], lambda k: wo_hl[:, LOP, k, :],
                      3 * KC if m == 0 else None).then_inc(wo_done, 1)

            def turn_x1(m):
                pe.wait_ge(x1_ready, m + 1)
                at_least(pe, logits_read, m)
                at_least(pe, place_read, min(m // TPB, NB - 2))
                for k in range(KC):
                    last = nc.tensor.transpose(ps[:, B_X1, k * P:(k + 1) * P], acc[:, m, k * P:(k + 1) * P], ident)
                last.then_inc(x1tr_done, 1)

            def logits(m):
                pe.wait_ge(x1T_ready, m + 1)
                to = ps[:, B_X1, 0:2 * E]
                for k in range(KC):
                    nc.tensor.matmul(to, rowT_hi[:, m % 2, k, :], gate_hl[:, k, :], start=(k == 0), stop=False)
                    last = nc.tensor.matmul(to, rowT_lo[:, m % 2, k, :], gate_hl[:, k, :], start=False,
                                            stop=(k == KC - 1))
                last.then_inc(logits_done, 1)

            def places(b):
                at, bank = slice(TPB * b, TPB * b + TPB), place_bank(b)
                pe.wait_ge(chosen_ready, (TPB + 1) * (b + 1))
                if bank != B_X1:
                    pe.wait_ge(kvbd_ready, 2 * HG * NB)
                    pe.wait_ge(place_read, b)
                    at_least(pe, plan_ready, b - NB + 2)
                    nc.tensor.matmul(ps[:, bank, COUNT], ones, earlier[:, TPB * b + TPB, :], start=True, stop=True)
                to = ps[:, bank, PLACE]
                nc.tensor.matmul(to, tri, chosen[:, at, :].rearrange("p t e -> p (t e)"), start=True, stop=False)
                nc.tensor.matmul(to, ones, earlier[:, at, :].rearrange("p t e -> p (t e)"), start=False, stop=True)\
                    .then_inc(place_done, 1)

            pe.wait_ge(cst_in, 16)
            for name, b, i in TODO:
                m = TPB * b + i
                if name in ("K", "V", "Q"):
                    project(b, name, i)
                elif name == "kv":
                    kv(b, i)
                elif name == "out":
                    attend(b, m, i)
                elif name == "tr":
                    turn(m)
                elif name == "wo":
                    output(m)
                elif name == "xt":
                    turn_x1(m)
                elif name == "lg":
                    if m == 0:
                        pe.wait_ge(gate_ready, 1)
                    logits(m)
                elif name == "rt":
                    places(b)

            def turn_rows(s, q, nth):
                pe.wait_ge(rows_in[q], 16 * nth)
                if not isinstance(s, int) or s >= 2:
                    pe.wait_ge(rowT_ready, s - 1)
                for k in range(KC):
                    last = nc.tensor.transpose(ps[:, 6 + q % 2, k * P:(k + 1) * P], rows[:, q, k * P:(k + 1) * P],
                                               ident)
                last.then_inc(rowtr_done, 1)

            def expert(s, q):
                e = pe.value_load(plan[0:1, 0, s:s + 1] if isinstance(s, int) else plan[0:1, 0, ds(s, 1)],
                                  min_val=0, max_val=E - 1)
                pe.wait_ge(ew_ready, e * KC + KC)
                pe.wait_ge(rowT_ready, s + 1)
                if not isinstance(s, int) or s >= 2:
                    pe.wait_ge(y_used, s - 1)
                three(ps[:, q, :], lambda k: rowT_hi[:, q, k, :], lambda k: rowT_lo[:, q, k, :],
                      lambda k: ew[:, ds(e, 1), HIP, k, :], lambda k: ew[:, ds(e, 1), LOP, k, :]).then_inc(y_done, 1)

            def turn_gates():
                pe.wait_ge(gate4_ready, 3)
                for q in range(NT // 4):
                    last = nc.tensor.transpose(ps[:, 5, q * P:(q + 1) * P],
                                               gate4[:, 4 * q:4 * q + 4, :].rearrange("p t r -> p (t r)").bitcast(F32),
                                               ident)
                last.then_inc(gtr_done, 1)

            def bias_of(t):
                at_least(pe, bias_used, t - 3)
                here = slice(t % 4 * 32, t % 4 * 32 + 32)
                nc.tensor.matmul(ps[:, bias_bank(t), :], gT[here, t // 4, :], bias_rows[here, :],
                                 start=True, stop=True).then_inc(bias_done, 1)

            pe.wait_ge(plan_ready, 1)
            turn_rows(0, 0, 1)
            pe.wait_ge(logits_read, NT)
            turn_rows(1, 1, 1)
            for s in range(FIRST):
                if s:
                    turn_rows(s + 1, (s + 1) % RING, (s + 1) // RING + 1)
                expert(s, s % 2)
                if s == PLACES_AT:
                    places(NB - 1)
                if s == TURN_AT:
                    turn_gates()
                for t in bias_tiles(s):
                    if t == 0:
                        pe.wait_ge(bias_ready, 1)
                        pe.wait_ge(gT_ready, 1)
                    bias_of(t)
            pe.wait_ge(plan_ready, 2)
            with pe.Fori(FIRST // RING, NS // RING) as j:
                for q in range(RING):
                    turn_rows(RING * j + (q + 1), (q + 1) % RING, j + ((q + 1) // RING + 1))
                    expert(RING * j + q, q % 2)
            for s in range(NS // RING * RING, NS):
                if s + 1 < NS:
                    turn_rows(s + 1, (s + 1) % RING, (s + 1) // RING + 1)
                expert(s, s % 2)


_INS = ["x", "xT", "wkT", "wvT", "wqT", "woT", "gateT", "expert_w", "expert_b", "consts", "no_entries", "entries"]


def kernel(L0_attn_x, L0_attn_cos, L0_attn_sin, L0_attn_Wq, L0_attn_Wk, L0_attn_Wv, L0_attn_Wo,
           L0_ffn_gate_w, L0_ffn_expert_w, L0_ffn_expert_b):
    import numpy as np
    import concourse.bacc as bacc
    from concourse.bass_utils import run_bass_kernel_spmd

    x = np.asarray(L0_attn_x)
    B, T, C = x.shape
    rows = np.ascontiguousarray(x.reshape(B * T, C))

    def by_block(w):
        w = np.asarray(w)
        return np.ascontiguousarray(w.reshape(w.shape[0], C // P, P).transpose(2, 1, 0))

    E = N_EXPERTS
    part, f32 = np.arange(P), np.float32
    consts = np.zeros((P, C_END), f32)
    consts[:, COL["IDENT"]] = np.eye(P, dtype=f32)
    consts[:, COL["TRI"]] = part[:, None] < part[None, :]
    consts[:, COL["ONES"]] = 1
    consts[:, COL["RANK"]] = np.tile(np.arange(E, 0, -1), 4)
    consts[:, COL["EBASE"]] = np.tile(np.arange(E) * REGION, 4)
    consts[:, COL["BEFORE"]] = (np.arange(E)[None, :] < np.arange(E)[:, None]).reshape(-1)
    consts[:, COL["SLOT"]] = np.arange(NS)
    consts[:, COL["SLOTROW"]] = np.arange(NS) * P
    consts[:, COL["HI"]] = part[:, None] // E % 2 == 0
    consts[:, COL["LO"]] = part[:, None] // E % 2 == 1
    consts[:, COL["HALF"]] = -0.5
    no_entries = np.zeros((TABLE, ENTRY), np.int32)
    no_entries[:, 2] = TOP * N_TOKENS + np.arange(TABLE)
    entries = np.zeros((P, NT, TOP, ENTRY), np.int32)
    entries[..., 0] = (np.arange(NT)[None, :] * P + part[:, None])[:, :, None]
    entries[..., 2] = entries[..., 0] * TOP + np.arange(TOP)
    arrays = {
        "x": rows,
        "xT": np.ascontiguousarray(rows.reshape(-1, P, C // P, P).transpose(0, 3, 2, 1)).reshape(-1, P, C),
        "wkT": by_block(L0_attn_Wk), "wvT": by_block(L0_attn_Wv),
        "wqT": by_block(L0_attn_Wq), "woT": by_block(L0_attn_Wo),
        "gateT": by_block(L0_ffn_gate_w),
        "expert_w": np.asarray(L0_ffn_expert_w), "expert_b": np.asarray(L0_ffn_expert_b),
        "consts": consts,
        "no_entries": no_entries,
        "entries": entries,
    }
    nc = bacc.Bacc("TRN2", target_bir_lowering=False, num_devices=1)
    args = [nc.dram_tensor(n, arrays[n].shape, I32 if n in ("no_entries", "entries") else F32, kind="ExternalInput").ap()
            for n in _INS]
    out = nc.dram_tensor("out", rows.shape, F32, kind="ExternalOutput").ap()
    build(nc, *args, out)
    r = run_bass_kernel_spmd(nc, [arrays], core_ids=[0])
    return r.results[0]["out"].reshape(B, T, C)
```
